# Optimizing a Trainium2 kernel written in Bass

```python
import numpy as np
import jax
import jax.numpy as jnp

def _softmax(x, axis=-1):
    return jax.nn.softmax(x, axis=axis)

def _gelu(x):
    return jax.nn.gelu(x, approximate=True)

def _silu(x):
    return jax.nn.silu(x)

def _sigmoid(x):
    return jax.nn.sigmoid(x)

def _layernorm(x, axis=-1, eps=1e-05):
    m = jnp.mean(x, axis=axis, keepdims=True)
    v = jnp.var(x, axis=axis, keepdims=True)
    return (x - m) / jnp.sqrt(v + eps)

def _scatter_add(tgt, idx, src, axis=0):
    return tgt.at[idx].add(src)

def _segment_sum(src, seg, n):
    return jax.ops.segment_sum(src, seg, n)
kernel_name = 'mk_seq_postln_d1_jaxref_r8_77414c'

def setup_inputs(seed: int=0):
    np.random.seed(seed)
    _w = jnp.asarray

    def _L0_attn_setup():
        import math
        import jax, jax.numpy as jnp
        import numpy as np
        EMBED_DIM = 128
        NUM_HEADS = 16
        HEAD_DIM = EMBED_DIM // NUM_HEADS

        def _xavier(key, fan_in, fan_out):
            lim = math.sqrt(6.0 / (fan_in + fan_out))
            return jax.random.uniform(key, (fan_out, fan_in), jnp.float32, -lim, lim)
        key = jax.random.key(seed)
        kx, kq, kk, kv, ko = jax.random.split(key, 5)
        B, L = (4, 256)
        x = jax.random.normal(kx, (B, L, EMBED_DIM), jnp.float32)
        return {'x': x, 'wq': _xavier(kq, EMBED_DIM, EMBED_DIM), 'bq': jnp.zeros((EMBED_DIM,), jnp.float32), 'wk': _xavier(kk, EMBED_DIM, EMBED_DIM), 'bk': jnp.zeros((EMBED_DIM,), jnp.float32), 'wv': _xavier(kv, EMBED_DIM, EMBED_DIM), 'bv': jnp.zeros((EMBED_DIM,), jnp.float32), 'wo': _xavier(ko, EMBED_DIM, EMBED_DIM), 'bo': jnp.zeros((EMBED_DIM,), jnp.float32)}
    _L0_attn_in = _L0_attn_setup()

    def _L0_ffn_setup():
        import jax, jax.numpy as jnp
        import numpy as np
        D_IN, D_HID = (128, 512)

        def _ternary(key, shape):
            return jax.random.randint(key, shape, -1, 2).astype(jnp.float32)

        def _tlin(x, w, s):
            return jnp.einsum('bsi,oi->bso', x, w) * s
        key = jax.random.key(seed)
        ks = jax.random.split(key, 12)
        inv = lambda fan: 1.0 / np.sqrt(fan).astype(np.float32)
        return {'x': jax.random.normal(ks[0], (4, 256, D_IN), dtype=jnp.float32), 'w1_w': _ternary(ks[1], (D_HID, D_IN)), 'w1_s': jax.random.uniform(ks[2], (D_HID,), dtype=jnp.float32) * inv(D_IN), 'w2_w': _ternary(ks[3], (D_HID, D_IN)), 'w2_s': jax.random.uniform(ks[4], (D_HID,), dtype=jnp.float32) * inv(D_IN), 'h1_w': _ternary(ks[5], (D_HID, D_HID)), 'h1_s': jax.random.uniform(ks[6], (D_HID,), dtype=jnp.float32) * inv(D_HID), 'h2_w': _ternary(ks[7], (D_HID, D_HID)), 'h2_s': jax.random.uniform(ks[8], (D_HID,), dtype=jnp.float32) * inv(D_HID), 'w3_w': _ternary(ks[9], (D_IN, D_HID)), 'w3_s': jax.random.uniform(ks[10], (D_IN,), dtype=jnp.float32) * inv(D_HID)}
    _L0_ffn_in = _L0_ffn_setup()
    _d = {'L0_attn_x': _L0_attn_in['x'], 'L0_attn_wq': _L0_attn_in['wq'], 'L0_attn_bq': _L0_attn_in['bq'], 'L0_attn_wk': _L0_attn_in['wk'], 'L0_attn_bk': _L0_attn_in['bk'], 'L0_attn_wv': _L0_attn_in['wv'], 'L0_attn_bv': _L0_attn_in['bv'], 'L0_attn_wo': _L0_attn_in['wo'], 'L0_attn_bo': _L0_attn_in['bo'], 'L0_ffn_w1_w': _L0_ffn_in['w1_w'], 'L0_ffn_w1_s': _L0_ffn_in['w1_s'], 'L0_ffn_w2_w': _L0_ffn_in['w2_w'], 'L0_ffn_w2_s': _L0_ffn_in['w2_s'], 'L0_ffn_h1_w': _L0_ffn_in['h1_w'], 'L0_ffn_h1_s': _L0_ffn_in['h1_s'], 'L0_ffn_h2_w': _L0_ffn_in['h2_w'], 'L0_ffn_h2_s': _L0_ffn_in['h2_s'], 'L0_ffn_w3_w': _L0_ffn_in['w3_w'], 'L0_ffn_w3_s': _L0_ffn_in['w3_s']}
    _x0 = _d['L0_attn_x']
    _d['L0_attn_x'] = jax.random.normal(jax.random.fold_in(jax.random.key(seed), 1), (2, 1024, 128), dtype=_x0.dtype)
    del _x0
    return _d

def reference(L0_attn_x, L0_attn_wq, L0_attn_bq, L0_attn_wk, L0_attn_bk, L0_attn_wv, L0_attn_bv, L0_attn_wo, L0_attn_bo, L0_ffn_w1_w, L0_ffn_w1_s, L0_ffn_w2_w, L0_ffn_w2_s, L0_ffn_h1_w, L0_ffn_h1_s, L0_ffn_h2_w, L0_ffn_h2_s, L0_ffn_w3_w, L0_ffn_w3_s):

    def _L0_attn_ref(x, wq, bq, wk, bk, wv, bv, wo, bo):
        import math
        import jax, jax.numpy as jnp
        import numpy as np
        EMBED_DIM = 128
        NUM_HEADS = 16
        HEAD_DIM = EMBED_DIM // NUM_HEADS

        def _xavier(key, fan_in, fan_out):
            lim = math.sqrt(6.0 / (fan_in + fan_out))
            return jax.random.uniform(key, (fan_out, fan_in), jnp.float32, -lim, lim)
        B, L, D = x.shape
        H, Dh = (NUM_HEADS, HEAD_DIM)

        def proj(w, b):
            return (jnp.einsum('bld,ed->ble', x, w) + b).reshape(B, L, H, Dh).transpose(0, 2, 1, 3)
        q, k, v = (proj(wq, bq), proj(wk, bk), proj(wv, bv))
        scale = 1.0 / math.sqrt(H)
        scores = jnp.einsum('bhqd,bhkd->bhqk', q, k) * scale
        attn = jax.nn.softmax(scores, axis=-1)
        out = jnp.einsum('bhqk,bhkd->bhqd', attn, v)
        out = out.transpose(0, 2, 1, 3).reshape(B, L, D)
        return jnp.einsum('bld,ed->ble', out, wo) + bo

    def _L0_ffn_ref(x, w1_w, w1_s, w2_w, w2_s, h1_w, h1_s, h2_w, h2_s, w3_w, w3_s):
        import jax, jax.numpy as jnp
        import numpy as np
        D_IN, D_HID = (128, 512)

        def _ternary(key, shape):
            return jax.random.randint(key, shape, -1, 2).astype(jnp.float32)

        def _tlin(x, w, s):
            return jnp.einsum('bsi,oi->bso', x, w) * s
        h = jax.nn.silu(_tlin(x, w1_w, w1_s)) * _tlin(x, w2_w, w2_s)
        h = jax.nn.gelu(_tlin(h, h1_w, h1_s), approximate=False)
        h = jax.nn.gelu(_tlin(h, h2_w, h2_s), approximate=False)
        return _tlin(h, w3_w, w3_s)
    x = L0_attn_x
    x = _layernorm(x + _L0_attn_ref(x, L0_attn_wq, L0_attn_bq, L0_attn_wk, L0_attn_bk, L0_attn_wv, L0_attn_bv, L0_attn_wo, L0_attn_bo), axis=-1)
    x = _layernorm(x + _L0_ffn_ref(x, L0_ffn_w1_w, L0_ffn_w1_s, L0_ffn_w2_w, L0_ffn_w2_s, L0_ffn_h1_w, L0_ffn_h1_s, L0_ffn_h2_w, L0_ffn_h2_s, L0_ffn_w3_w, L0_ffn_w3_s), axis=-1)
    return x

_drawn_inputs = setup_inputs


def setup_inputs(seed=0):
    import zlib

    import numpy as np

    out = dict(_drawn_inputs(seed))
    spreads = {'L0_attn_bq': (0.0, 0.8),
     'L0_attn_bk': (0.0, 0.8),
     'L0_attn_bv': (0.0, 0.1),
     'L0_attn_bo': (0.0, 0.1)}
    factors = {'L0_ffn_w1_w': 8.0,
     'L0_ffn_w1_s': 8.0,
     'L0_ffn_w2_w': 8.0,
     'L0_ffn_w2_s': 8.0,
     'L0_ffn_h1_w': 8.0,
     'L0_ffn_h1_s': 8.0,
     'L0_ffn_h2_w': 8.0,
     'L0_ffn_h2_s': 8.0,
     'L0_ffn_w3_w': 8.0,
     'L0_ffn_w3_s': 8.0}
    for name, (base, spread) in spreads.items():
        noise = np.random.default_rng([zlib.crc32(name.encode()), seed]).standard_normal(out[name].shape)
        drawn = base * np.exp(spread * noise) if base else spread * noise
        out[name] = jnp.asarray(drawn.astype(out[name].dtype))
    for name, factor in factors.items():
        out[name] = (out[name] * factor).astype(out[name].dtype)
    return out
```

```python
from contextlib import ExitStack

import concourse.bass as bass
from concourse import mybir

ALU = mybir.AluOpType
ACT = mybir.ActivationFunctionType
AX = mybir.AxisListType
F32 = mybir.dt.float32
BF16 = mybir.dt.bfloat16

P = 128
B, L, D = 2, 1024, 128
H, DH = 16, 8
HID = 512
TOK = B * L
SCALE = 1.0 / H ** 0.5
EPS = 1e-5

C = 512
NC_ = TOK // C
HG = 4
NG = H // HG
G_ALL = B * NG
QC = L // C
U_ALL = G_ALL * QC
KT = L // P
PARTS = 3
ROWS = DH * PARTS * PARTS
MROWS = ROWS + PARTS
QT = C // P
TURNS = HG * QT
LEAD = 4
TSTEP = 6
PER = 4
STEPS = PER * KT
ITERS = U_ALL // PER
LOAD_INC = 16 * 2 * PARTS * PARTS
MROW_INC = 16 * PARTS
MT = HID // P
TILES = C // P

ST_BANK, MAX_BANK, PV_BANK, T_BANK = 0, 2, 6, 7
JOB_BANKS = [0, 1, 6, 7]
WO_BANK, X1T_BANK, W3_BANK = 6, 7, 4

JOBS = [("k", 0), ("k", 1), ("q", 0), ("q", 1), ("k", 2), ("k", 3), ("q", 2), ("q", 3)]


def build(nc, xT, x, wqT, wkT, wvT, woT, bq, bk, bv, bo, w1T, w2T, h1T, h2T, w3T,
          w1s, w2s, h1s, h2s, w3s, parts_dram, out):
    with ExitStack() as ctx:
        def sb(name, shape, dt=F32):
            return ctx.enter_context(nc.sbuf_tensor(name, shape, dt))

        def sem(name):
            return ctx.enter_context(nc.semaphore(name))

        xT_sb = sb("xT_sb", [P, TOK])
        xres = sb("xres", [P, TOK // P, D])
        wq_sb, wk_sb, wv_sb = (sb(f"w{n}_sb", [P, D]) for n in "qkv")
        wo_sb = sb("wo_sb", [P, NG, D])
        w1_sb, w2_sb = sb("w1_sb", [P, HID]), sb("w2_sb", [P, HID])
        h1_sb, h2_sb = sb("h1_sb", [P, MT, HID]), sb("h2_sb", [P, MT, HID])
        w3_sb = sb("w3_sb", [P, MT, D])
        bq_sb, bk_sb = sb("bq_sb", [P, 1]), sb("bk_sb", [P, 1])
        bv_bc, bo_bc, s3_bc = (sb(n, [P, D]) for n in ("bv_bc", "bo_bc", "s3_bc"))
        s_sb = {n: sb(f"{n}_sb", [P, MT]) for n in ("w1s", "w2s", "h1s", "h2s")}
        ident, ident_bf = sb("ident", [P, P]), sb("ident_bf", [P, P], BF16)

        qk = sb("qk", [P, 4 * HG * L], BF16)
        qx = qk[:, 0:2 * HG * L].rearrange("p (s c h t) -> p s c h t", s=2, c=QC, h=HG)
        kx = qk[:, 2 * HG * L:4 * HG * L].rearrange("p (s c h t) -> p s c h t", s=2, c=QC, h=HG)
        attn = sb("attn", [P, U_ALL, C])
        hid = [qk[:, :].bitcast(F32).rearrange("p (m t) -> p m t", m=MT),
               attn[:, :, :].rearrange("p u c -> p (u c)").rearrange("p (m t) -> p m t", m=MT)]
        proj = sb("proj", [P, len(JOBS), C])
        prt = sb("prt", [P, 2 * PARTS * TOK], BF16)
        part = {n: prt[:, a * PARTS * TOK:(a + 1) * PARTS * TOK].rearrange("p (i t) -> p i t", i=PARTS)
                for a, n in enumerate("qk")}
        later = prt[:, :].bitcast(F32)
        den = [proj[:, :, :], later[:, 0:8 * C].rearrange("p (u c) -> p u c", c=C)]
        x1T = later[:, 8 * C:12 * C]
        v_sb = sb("v_sb", [P, G_ALL, KT, HG * DH])
        v_pad = sb("v_pad", [P, 2, KT, HG, 32])
        probs = sb("probs", [P, 2, HG, C])
        negmax = sb("negmax", [P, 2, TURNS])
        zeros = sb("zeros", [P, TURNS])
        mrest = sb("mrest", [P, TURNS])
        mpart = sb("mpart", [P, 2, P // TURNS, TURNS], BF16)
        mT = sb("mT", [P, 2, P], BF16)
        x1 = sb("x1", [P, TOK // P, D])
        gate = sb("gate", [P, 2, C])
        z = sb("z", [P, 2, TILES, D])
        stats, mv = sb("stats", [P, TILES, 6]), sb("mv", [P, 2, TILES, 2])
        veps, rstd, power = sb("veps", [P, TILES]), sb("rstd", [P, 2, TILES]), sb("power", [P, TILES])
        ps = ctx.enter_context(nc.psum_tensor("ps", [P, 8, C], F32))
        ps_t = ps[:, T_BANK, :].bitcast(BF16)[:, 0:P]

        in_x = [sem(f"in_x{c}") for c in range(NC_)]
        in_k, in_q, in_v = sem("in_k"), sem("in_q"), sem("in_v")
        in_mid = sem("in_mid")
        in_ffn = sem("in_ffn")
        ones_set = sem("ones_set")
        ident_ready = sem("ident_ready")
        job_done = sem("job_done")
        v_proj = sem("v_proj")
        proj_ready = sem("proj_ready")
        split_act = sem("split_act")
        split_dve = sem("split_dve")
        split_pool = sem("split_pool")
        v_ready = sem("v_ready")
        parts_out = [sem(f"parts_out{b}") for b in range(B)]
        rows_in = [sem(f"rows_in{s}") for s in range(2)]
        v_staged = sem("v_staged")
        max_scores = sem("max_scores")
        max_taken = sem("max_taken")
        msplit_step = sem("msplit_step")
        max_split = sem("max_split")
        max_turned = sem("max_turned")
        max_copied = sem("max_copied")
        mrow_in = [sem(f"mrow_in{s}") for s in range(2)]
        scores = sem("scores")
        exp_done = sem("exp_done")
        pv_done = sem("pv_done")
        unit_out = sem("unit_out")
        den_set = [sem(f"den_set{b}") for b in range(B)]
        DEN = [(0, 0, 8), (1, 0, 6), (1, 6, 7), (1, 7, 8)]
        den_in = [sem(f"den_in{n}") for n in range(len(DEN))]
        xres_ready = sem("xres_ready")
        w3_ready = sem("w3_ready")
        normed = sem("normed")
        chunk_normed = sem("chunk_normed")
        wo_done = sem("wo_done")
        z_ready = sem("z_ready")
        stats_ready = sem("stats_ready")
        var_ready = sem("var_ready")
        pow_step = sem("pow_step")
        rstd_ready = sem("rstd_ready")
        x1_ready = sem("x1_ready")
        x1_turned = sem("x1_turned")
        x1T_ready = sem("x1T_ready")
        gate_mm = sem("gate_mm")
        act_tile = sem("act_tile")
        h0_ready = sem("h0_ready")
        gelu_mm = sem("gelu_mm")
        w3_done = sem("w3_done")
        out_ready = sem("out_ready")
        out_in = sem("out_in")

        block = ctx.enter_context(nc.Block())

        def den_rows(b, j, u0, u1):
            src = attn[32 * j + DH:32 * j + 2 * DH, b * 8 + u0:b * 8 + u1, :]
            return den[b][32 * j:32 * j + DH, u0:u1, :], src

        @block.sync
        def _(sp):
            xT_c = xT.rearrange("p (c t) -> c p t", c=NC_)
            sp.dma_start(wk_sb[:], wkT).then_inc(in_k, 16)
            sp.dma_start(bk_sb[:], bk).then_inc(in_k, 16)
            sp.dma_start(xT_sb[:, 0:C], xT_c[0]).then_inc(in_x[0], 16)
            sp.dma_start(wq_sb[:], wqT).then_inc(in_q, 16)
            sp.dma_start(bq_sb[:], bq).then_inc(in_q, 16)
            for c in range(2, NC_):
                sp.dma_start(xT_sb[:, c * C:(c + 1) * C], xT_c[c]).then_inc(in_x[c], 16)
            sp.dma_start(wv_sb[:], wvT).then_inc(in_v, 16)
            sp.dma_start(bv_bc[:], bv.partition_broadcast(P)).then_inc(in_v, 16)

            def store_parts(n):
                name, c = JOBS[n]
                b, qc = c // QC, c % QC
                for i in range(PARTS):
                    sp.dma_start(parts_dram[name][i, :, qc, b * NG:(b + 1) * NG]
                                 .rearrange("d g h t -> (g h) d t"),
                                 part[name][:, i, c * C:(c + 1) * C]).then_inc(parts_out[b], 16)

            def load_rows(g, slot):
                for n, dst in (("k", kx), ("q", qx)):
                    src = parts_dram[n].rearrange("i d c g h t -> i d c g (h t)")
                    for i in range(PARTS):
                        for j in range(PARTS):
                            r = DH * (i * PARTS + j)
                            sp.dma_start(dst[r:r + DH, slot].rearrange("d c h t -> d c (h t)"),
                                         src[i if n == "q" else j, :, :, bass.ds(g, 1), :]
                                         .rearrange("d c o t -> d c (o t)"))\
                              .then_inc(rows_in[slot], 16)

            def load_max(i, w):
                slot, qc = w // QC % 2, w % QC
                sp.wait_ge(max_copied, i * PER + w + 1)
                for n in range(PARTS):
                    sp.dma_start(qx[ROWS + n:ROWS + n + 1, slot, qc, :, :].rearrange("o h t -> o (h t)"),
                                 mT[n * TURNS:(n + 1) * TURNS, w % 2, :])\
                      .then_inc(mrow_in[w % 2], 16)

            sp.wait_ge(ones_set, 1)
            for n in range(4):
                sp.wait_ge(split_dve, 4 * n + 4)
                store_parts(n)
            sp.wait_ge(parts_out[0], 4 * PARTS * 16)
            load_rows(0, 0)
            load_rows(1, 1)
            load_max(0, 0)
            for n in range(4, 8):
                sp.wait_ge(split_pool, 3 * (n - 4) + 3)
                store_parts(n)
            sp.wait_ge(parts_out[1], 4 * PARTS * 16)

            def units(i, last):
                load_max(i, 1)
                load_max(i, 2)
                if not last:
                    sp.wait_ge(scores, i * (STEPS * HG) + STEPS * HG // 2)
                    load_rows(i * 2 + 2, 0)
                load_max(i, 3)
                if not last:
                    load_max(i, 4)
                    sp.wait_ge(scores, i * (STEPS * HG) + STEPS * HG)
                    load_rows(i * 2 + 3, 1)

            with sp.Fori(0, ITERS - 1) as i:
                units(i, False)
            for n, dst, src in ((in_ffn, w1_sb[:], w1T), (in_ffn, w2_sb[:], w2T),
                                (in_ffn, h1_sb[:], h1T.rearrange("(k p) o -> p k o", p=P)),
                                (in_ffn, h2_sb[:], h2T.rearrange("(k p) o -> p k o", p=P)),
                                (in_ffn, w3_sb[:], w3T.rearrange("(k p) o -> p k o", p=P)),
                                (in_ffn, s3_bc[:], w3s.partition_broadcast(P)),
                                (in_ffn, s_sb["w1s"][:], w1s), (in_ffn, s_sb["w2s"][:], w2s),
                                (in_ffn, s_sb["h1s"][:], h1s), (in_ffn, s_sb["h2s"][:], h2s)):
                sp.dma_start(dst, src).then_inc(n, 16)
            units(ITERS - 1, True)
            for n, (b, u0, u1) in enumerate(DEN):
                sp.wait_ge(den_set[b], 1)
                sp.wait_ge(unit_out, b * 8 + u1)
                for j in range(HG):
                    dst, src = den_rows(b, j, u0, u1)
                    sp.dma_start(dst, src).then_inc(den_in[n], 16)
            out_c = out.rearrange("(c t p) d -> c p t d", p=P, t=TILES)
            for c in range(NC_):
                sp.wait_ge(out_ready, c + 1)
                sp.dma_start(out_c[c], xres[:, c * TILES:(c + 1) * TILES, :]).then_inc(out_in, 16)
            sp.wait_ge(out_in, 16 * NC_)

        @block.scalar
        def _(act):
            xT_c = xT.rearrange("p (c t) -> c p t", c=NC_)
            act.dma_start(xT_sb[:, C:2 * C], xT_c[1]).then_inc(in_x[1], 16)
            act.dma_start(xres[:], x.rearrange("(t p) d -> p t d", p=P)).then_inc(in_mid, 16)
            act.dma_start(bo_bc[:], bo.partition_broadcast(P)).then_inc(in_mid, 16)
            act.wait_ge(ones_set, 2)
            for j in range(HG):
                act.dma_start(wo_sb[32 * j:32 * j + DH, :, :],
                              woT.rearrange("(g j d) e -> j d g e", g=NG, j=HG)[j]).then_inc(in_mid, 16)
            act.wait_ge(in_k, 32)
            act.wait_ge(in_q, 32)
            for n, (name, c) in enumerate(JOBS):
                act.wait_ge(job_done, n + 1)
                nc.scalar.activation(proj[:, n, :], ps[:, JOB_BANKS[n % 4], :], ACT.Identity,
                                     bias=(bq_sb if name == "q" else bk_sb)[:, 0:1]).then_inc(proj_ready, 1)
                act.wait_ge(proj_ready, n + 1)
                if n >= 4:
                    nc.scalar.activation(part[name][:, 0, c * C:(c + 1) * C], proj[:, n, :],
                                         ACT.Copy).then_inc(split_act, 1)

            def exps(i, k):
                for h in range(HG):
                    act.wait_ge(scores, i * (STEPS * HG) + k * HG + h + 1)
                    nc.scalar.activation(probs[:, k % 2, h, :], ps[:, ST_BANK + h % 2, :], ACT.Exp,
                                         scale=SCALE).then_inc(exp_done, 1)

            attn_flat = attn[:, :, :].rearrange("p u c -> p (u c)")

            def units(i, last):
                for k in range(STEPS):
                    if not (last and k == STEPS - 1):
                        exps(i, k + 1)
                    if k % KT == KT - 1:
                        act.wait_ge(pv_done, i * STEPS + k + 1)
                        nc.scalar.activation(attn_flat[:, bass.ds(i * (PER * C) + k // KT * C, C)],
                                             ps[:, PV_BANK, :], ACT.Copy).then_inc(unit_out, 1)

            exps(0, 0)
            with act.Fori(0, ITERS - 1) as i:
                units(i, False)
            units(ITERS - 1, True)

            act.wait_ge(in_ffn, 160)
            for c in range(NC_):
                act.wait_ge(x1_turned, c + 1)
                nc.scalar.activation(x1T[:, c * C:(c + 1) * C], ps[:, X1T_BANK, :], ACT.Copy)\
                  .then_inc(x1T_ready, 1)
                for m in range(MT):
                    n = c * MT + m
                    act.wait_ge(gate_mm, n + 1)
                    if n >= 2:
                        act.wait_ge(h0_ready, n - 1)
                    nc.scalar.activation(gate[:, n % 2, :], ps[:, 2 * (n % 2), :], ACT.Silu,
                                         scale=s_sb["w1s"][:, m:m + 1]).then_inc(act_tile, 1)
            for layer, scale in enumerate(("h1s", "h2s")):
                dst = hid[1 - layer]

                def chunk(c):
                    for m in range(MT):
                        act.wait_ge(gelu_mm, c * MT + layer * (NC_ * MT) + m + 1)
                        nc.scalar.activation(dst[:, m, bass.ds(c * C, C)], ps[:, m, :], ACT.Gelu,
                                             scale=s_sb[scale][:, m:m + 1]).then_inc(act_tile, 1)

                with act.Fori(0, NC_) as c:
                    chunk(c)

        @block.gpsimd
        def _(pool):
            nc.gpsimd.memset(kx[64:MROWS, :, :, :, :], 1.0).then_inc(ones_set, 1)
            pool.wait_ge(ones_set, 1)
            nc.gpsimd.memset(wo_sb[:], 0.0).then_inc(ones_set, 1)
            nc.gpsimd.memset(ident[:], 1.0).then_inc(ident_ready, 1)
            pool.wait_ge(ident_ready, 1)
            nc.gpsimd.affine_select(out=ident[:], in_=ident[:], compare_op=ALU.is_equal, fill=0.0, base=0,
                                    pattern=[[-1, P]], channel_multiplier=1).then_inc(ident_ready, 1)
            pool.wait_ge(ident_ready, 2)
            nc.gpsimd.tensor_copy(ident_bf[:], ident[:]).then_inc(ident_ready, 1)
            nc.gpsimd.memset(power[:], -0.5).then_inc(ones_set, 1)
            nc.gpsimd.memset(v_pad[:], 1.0).then_inc(ones_set, 1)
            nc.gpsimd.memset(mpart[:], 0.0).then_inc(ones_set, 1)
            nc.gpsimd.memset(zeros[:], 0.0).then_inc(ones_set, 1)
            pool.wait_ge(ones_set, 6)

            def stage_v(g, slot):
                nc.gpsimd.tensor_copy(
                    v_pad[:, slot, :, :, 0:DH],
                    v_sb[:, :, :, :].rearrange("p g k (h d) -> p (g k) h d", h=HG)[:, bass.ds(g * KT, KT), :, :]
                ).then_inc(v_staged, 1)

            def split(n):
                name, c = JOBS[n]
                at = slice(c * C, (c + 1) * C)
                done = 3 * (n - 4)
                pool.wait_ge(split_act, n - 3)
                nc.gpsimd.tensor_tensor(proj[:, n, :], proj[:, n, :], part[name][:, 0, at],
                                        ALU.subtract).then_inc(split_pool, 1)
                pool.wait_ge(split_pool, done + 1)
                nc.gpsimd.tensor_copy(part[name][:, 1, at], proj[:, n, :]).then_inc(split_pool, 1)
                pool.wait_ge(split_pool, done + 2)
                nc.gpsimd.tensor_tensor(part[name][:, 2, at], proj[:, n, :], part[name][:, 1, at],
                                        ALU.subtract).then_inc(split_pool, 1)

            def split_max(i, w):
                m, parts = negmax[:, w % 2, :], mpart[:, w % 2, :, :]
                done = i * (3 * PER) + 3 * w
                pool.wait_ge(max_taken, i * (PER * TURNS) + w * TURNS + TURNS)
                nc.gpsimd.tensor_tensor(parts[:, 0, :], m, zeros[:], ALU.add).then_inc(msplit_step, 1)
                pool.wait_ge(msplit_step, done + 1)
                nc.gpsimd.tensor_tensor(mrest[:], m, parts[:, 0, :], ALU.subtract).then_inc(msplit_step, 1)
                pool.wait_ge(msplit_step, done + 2)
                nc.gpsimd.tensor_tensor(parts[:, 1, :], mrest[:], zeros[:], ALU.add)\
                  .then_inc(msplit_step, 1)
                pool.wait_ge(msplit_step, done + 3)
                nc.gpsimd.tensor_tensor(parts[:, 2, :], mrest[:], parts[:, 1, :], ALU.subtract)\
                  .then_inc(max_split, 1)

            split(4)
            split(5)
            pool.wait_ge(v_ready, 2)
            stage_v(0, 0)
            stage_v(1, 1)
            split_max(0, 0)
            split(6)
            split(7)
            pool.wait_ge(v_ready, NC_)

            def units(i, last):
                split_max(i, 1)
                split_max(i, 2)
                if not last:
                    pool.wait_ge(pv_done, i * STEPS + STEPS // 2)
                    stage_v(i * 2 + 2, 0)
                split_max(i, 3)
                if not last:
                    split_max(i, 4)
                    pool.wait_ge(pv_done, i * STEPS + STEPS)
                    stage_v(i * 2 + 3, 1)

            with pool.Fori(0, ITERS - 1) as i:
                units(i, False)
            pool.wait_ge(split_dve, 4 * 4)
            pool.wait_ge(split_pool, 3 * 4)
            for b in range(B):
                pool.wait_ge(parts_out[b], 4 * PARTS * 16)
            for b in range(B):
                nc.gpsimd.memset(den[b], 1.0).then_inc(den_set[b], 1)
            pool.wait_ge(in_mid, 96)
            nc.gpsimd.tensor_tensor(xres[:], xres[:], bo_bc[:, :].unsqueeze(1).broadcast_to([P, TOK // P, D]),
                                    ALU.add).then_inc(xres_ready, 1)
            pool.wait_ge(in_ffn, 160)
            nc.gpsimd.tensor_tensor(w3_sb[:], w3_sb[:], s3_bc[:, :].unsqueeze(1).broadcast_to([P, MT, D]),
                                    ALU.mult).then_inc(w3_ready, 1)
            units(ITERS - 1, True)
            for n in range(2 * NC_):
                pool.wait_ge(var_ready, n + 1)
                nc.gpsimd.tensor_scalar(veps[:], mv[:, n % 2, :, 1], EPS, None, ALU.add).then_inc(pow_step, 1)
                pool.wait_ge(pow_step, n + 1)
                nc.gpsimd.tensor_tensor(rstd[:, n % 2, :], veps[:], power[:], ALU.pow).then_inc(rstd_ready, 1)

        @block.vector
        def _(dve):
            def split(n):
                name, c = JOBS[n]
                at = slice(c * C, (c + 1) * C)
                done = 4 * n
                dve.wait_ge(proj_ready, n + 1)
                nc.vector.tensor_copy(part[name][:, 0, at], proj[:, n, :]).then_inc(split_dve, 1)
                dve.wait_ge(split_dve, done + 1)
                nc.vector.tensor_tensor(proj[:, n, :], proj[:, n, :], part[name][:, 0, at],
                                        ALU.subtract).then_inc(split_dve, 1)
                dve.wait_ge(split_dve, done + 2)
                nc.vector.tensor_copy(part[name][:, 1, at], proj[:, n, :]).then_inc(split_dve, 1)
                dve.wait_ge(split_dve, done + 3)
                nc.vector.tensor_tensor(part[name][:, 2, at], proj[:, n, :], part[name][:, 1, at],
                                        ALU.subtract).then_inc(split_dve, 1)

            for n in range(4):
                split(n)
            dve.wait_ge(in_v, 32)
            for c in range(NC_):
                dve.wait_ge(v_proj, c + 1)
                b, k0 = c // (NC_ // B), (c % (NC_ // B)) * TILES
                nc.vector.tensor_tensor(
                    v_sb[:, b * NG:(b + 1) * NG, k0:k0 + TILES, :],
                    ps[:, MAX_BANK + c, :].rearrange("p (t g e) -> p g t e", t=TILES, g=NG),
                    bv_bc[:, :].rearrange("p (g e) -> p g e", g=NG).unsqueeze(2)
                    .broadcast_to([P, NG, TILES, HG * DH]),
                    ALU.add).then_inc(v_ready, 1)

            def turn(i, t):
                dve.wait_ge(max_scores, i * (PER * TURNS) + t + 1)
                if t % TURNS == 0 and t >= 2 * TURNS:
                    dve.wait_ge(max_split, i * PER + t // TURNS - 1)
                bank = MAX_BANK + 2 * (t % 2)
                nc.vector.tensor_reduce(negmax[:, t // TURNS % 2, t % TURNS:t % TURNS + 1],
                                        ps[:, bank:bank + 2, :], AX.XY, ALU.max, negate=True)\
                  .then_inc(max_taken, 1)

            def copy_max(i, w):
                dve.wait_ge(max_turned, i * PER + w + 1)
                nc.vector.tensor_copy(mT[:, w % 2, :], ps_t).then_inc(max_copied, 1)

            for t in range(TURNS + LEAD):
                turn(0, t)
            copy_max(0, 0)

            def units(i, last):
                for k in range(STEPS):
                    for t in (TURNS + LEAD + 2 * k, TURNS + LEAD + 2 * k + 1):
                        if not (last and t >= PER * TURNS):
                            turn(i, t)
                    if k % KT == TSTEP and not (last and k // KT == PER - 1):
                        copy_max(i, k // KT + 1)

            with dve.Fori(0, ITERS - 1) as i:
                units(i, False)
            units(ITERS - 1, True)

            steps = [0]

            def norm(c):
                b, qc = c // QC, c % QC
                if c == 0:
                    dve.wait_ge(den_in[0], 64)
                if c == QC:
                    dve.wait_ge(den_in[1], 64)
                for g in range(NG):
                    u = g * QC + qc
                    if b == B - 1 and g == NG - 1:
                        dve.wait_ge(den_in[2 + qc], 64)
                    nc.vector.reciprocal(den[b][:, u, :], den[b][:, u, :]).then_inc(normed, 1)
                    steps[0] += 1
                    dve.wait_ge(normed, steps[0])
                    ins = nc.vector.tensor_tensor(attn[:, b * 8 + u, :], attn[:, b * 8 + u, :],
                                                  den[b][:, u, :], ALU.mult)
                ins.then_inc(chunk_normed, 1)

            def layernorm(n, psum, add, dst):
                zc, st, m = z[:, n % 2], stats, mv[:, n % 2]
                nc.vector.tensor_tensor(zc, psum.rearrange("p (t d) -> p t d", t=TILES), add, ALU.add)\
                  .then_inc(z_ready, 1)
                dve.wait_ge(z_ready, n + 1)
                for t in range(TILES):
                    ins = nc.vector.bn_stats(st[:, t, :], zc[:, t, :])
                ins.then_inc(stats_ready, 1)
                dve.wait_ge(stats_ready, n + 1)
                for t in range(TILES):
                    ins = nc.vector.bn_aggr(m[:, t, :], st[:, t, :])
                ins.then_inc(var_ready, 1)
                dve.wait_ge(rstd_ready, n + 1)
                for t in range(TILES):
                    ins = nc.vector.tensor_scalar(dst[:, t, :], zc[:, t, :], m[:, t, 0:1],
                                                  rstd[:, n % 2, t:t + 1], ALU.subtract, ALU.mult)
                return ins

            def gated(c):
                for m in range(MT):
                    n = c * MT + m
                    dve.wait_ge(act_tile, n + 1)
                    nc.vector.scalar_tensor_tensor(out=hid[0][:, m, c * C:(c + 1) * C],
                                                   in0=ps[:, 2 * (n % 2) + 1, :], scalar=s_sb["w2s"][:, m:m + 1],
                                                   in1=gate[:, n % 2, :], op0=ALU.mult, op1=ALU.mult)\
                      .then_inc(h0_ready, 1)

            def first(c):
                dve.wait_ge(wo_done, c + 1)
                if c == 0:
                    dve.wait_ge(xres_ready, 1)
                at = slice(c * TILES, (c + 1) * TILES)
                layernorm(c, ps[:, WO_BANK, :], xres[:, at, :], x1[:, at, :]).then_inc(x1_ready, 1)

            norm(0)
            norm(1)
            first(0)
            dve.wait_ge(in_ffn, 160)
            for c in range(1, NC_):
                if c + 1 < NC_:
                    norm(c + 1)
                first(c)
                gated(c - 1)
            gated(NC_ - 1)
            for c in range(NC_):
                dve.wait_ge(w3_done, c + 1)
                at = slice(c * TILES, (c + 1) * TILES)
                layernorm(NC_ + c, ps[:, W3_BANK + c % 2, :], x1[:, at, :], xres[:, at, :])\
                  .then_inc(out_ready, 1)

        @block.tensor
        def _(pe):
            for n, (name, c) in enumerate(JOBS):
                pe.wait_ge(in_x[c], 16)
                if n == 0:
                    pe.wait_ge(in_k, 32)
                if n == 2:
                    pe.wait_ge(in_q, 32)
                if n >= 4:
                    pe.wait_ge(proj_ready, n - 3)
                nc.tensor.matmul(ps[:, JOB_BANKS[n % 4], :], (wq_sb if name == "q" else wk_sb)[:],
                                 xT_sb[:, c * C:(c + 1) * C], start=True, stop=True).then_inc(job_done, 1)
                if n == 3:
                    pe.wait_ge(in_v, 32)
                    for c in range(NC_):
                        pe.wait_ge(in_x[c], 16)
                        for t in range(TILES):
                            ins = nc.tensor.matmul(ps[:, MAX_BANK + c, t * P:(t + 1) * P],
                                                   xT_sb[:, c * C + t * P:c * C + (t + 1) * P], wv_sb[:],
                                                   start=True, stop=True)
                        ins.then_inc(v_proj, 1)

            def turn(i, t, half):
                slot, qc, h, q = t // (QC * TURNS) % 2, t // TURNS % QC, t % TURNS // QT, t % QT
                if half == 0:
                    if t >= 2:
                        pe.wait_ge(max_taken, i * (PER * TURNS) + t - 1)
                    if t % (QC * TURNS) == 0:
                        pe.wait_ge(rows_in[slot], i * LOAD_INC + (t // (PER * TURNS) + 1) * LOAD_INC)
                ins = nc.tensor.matmul(ps[:, MAX_BANK + 2 * (t % 2) + half, :],
                                       qx[0:ROWS, slot, qc, h, q * P:(q + 1) * P],
                                       kx[0:ROWS, slot, half, h, :], start=True, stop=True)
                if half == 1:
                    ins.then_inc(max_scores, 1)

            def turn_max(i, w):
                pe.wait_ge(max_split, i * PER + w + 1)
                pe.wait_ge(max_copied, i * PER + w)
                nc.tensor.transpose(ps_t, mpart[:, w % 2, :, :].rearrange("p i t -> p (i t)"), ident_bf[:])\
                  .then_inc(max_turned, 1)

            def score(i, k, h):
                w, kt = k // KT, k % KT
                slot, qc = w // QC % 2, w % QC
                if k > 0 or h >= 2:
                    pe.wait_ge(exp_done, i * (STEPS * HG) + k * HG + h - 1)
                if kt == 0 and h == 0:
                    pe.wait_ge(mrow_in[w % 2], i * (PER // 2 * MROW_INC) + (w // 2 + 1) * MROW_INC)
                k0 = kt % TILES * P
                nc.tensor.matmul(ps[:, ST_BANK + h % 2, :], kx[0:MROWS, slot, kt // TILES, h, k0:k0 + P],
                                 qx[0:MROWS, slot, qc, h, :], start=True, stop=True)\
                  .then_inc(scores, 1)

            def product(i, k):
                w, kt = k // KT, k % KT
                if kt == 0 and w % QC == 0:
                    pe.wait_ge(v_staged, i * (PER // QC) + w // QC + 1)
                pe.wait_ge(exp_done, i * (STEPS * HG) + k * HG + HG + (kt == 0))
                for h in range(HG):
                    ins = nc.tensor.matmul(ps[32 * h:32 * h + 32, PV_BANK, :], v_pad[:, w // QC, kt, h, :],
                                           probs[:, k % 2, h, :], start=(kt == 0), stop=(kt == KT - 1),
                                           tile_position=(0, 32 * h))
                ins.then_inc(pv_done, 1)

            pe.wait_ge(v_ready, NC_)
            for t in range(TURNS + LEAD):
                turn(0, t, 0)
                turn(0, t, 1)
            pe.wait_ge(proj_ready, len(JOBS))
            pe.wait_ge(ident_ready, 3)
            turn_max(0, 0)
            for h in range(HG):
                score(0, 0, h)

            def units(i, last):
                for k in range(STEPS):
                    for h in range(HG):
                        if not (last and k == STEPS - 1):
                            score(i, k + 1, h)
                        t = TURNS + LEAD + 2 * k + h // 2
                        if not (last and t >= PER * TURNS):
                            turn(i, t, h % 2)
                    if k % KT == TSTEP and not (last and k // KT == PER - 1):
                        turn_max(i, k // KT + 1)
                    product(i, k)

            with pe.Fori(0, ITERS - 1) as i:
                units(i, False)
            units(ITERS - 1, True)

            def out_proj(c):
                b, qc = c // QC, c % QC
                pe.wait_ge(chunk_normed, c + 1)
                if c == 0:
                    pe.wait_ge(in_mid, 96)
                    pe.wait_ge(unit_out, U_ALL)
                if c >= 1:
                    pe.wait_ge(z_ready, c)
                for t in range(TILES):
                    for g in range(NG):
                        ins = nc.tensor.matmul(ps[:, WO_BANK, t * P:(t + 1) * P],
                                               attn[:, b * 8 + g * QC + qc, t * P:(t + 1) * P], wo_sb[:, g, :],
                                               start=(g == 0), stop=(g == NG - 1))
                ins.then_inc(wo_done, 1)

            def turn_x1(c):
                pe.wait_ge(x1_ready, c + 1)
                if c >= 1:
                    pe.wait_ge(x1T_ready, c)
                for t in range(TILES):
                    ins = nc.tensor.transpose(ps[:, X1T_BANK, t * P:(t + 1) * P], x1[:, c * TILES + t, :],
                                              ident[:])
                ins.then_inc(x1_turned, 1)

            def gate_products(c):
                if c == 0:
                    pe.wait_ge(in_ffn, 160)
                pe.wait_ge(x1T_ready, c + 1)
                for m in range(MT):
                    n = c * MT + m
                    if n >= 2:
                        pe.wait_ge(h0_ready, n - 1)
                    for a, w in enumerate((w1_sb, w2_sb)):
                        ins = nc.tensor.matmul(ps[:, 2 * (n % 2) + a, :], w[:, m * P:(m + 1) * P],
                                               x1T[:, c * C:(c + 1) * C], start=True, stop=True)
                    ins.then_inc(gate_mm, 1)

            out_proj(0)
            out_proj(1)
            turn_x1(0)
            gate_products(0)
            for c in range(1, NC_):
                if c + 1 < NC_:
                    out_proj(c + 1)
                turn_x1(c)
                gate_products(c)

            for layer, w in enumerate((h1_sb, h2_sb)):
                src = hid[layer]
                if layer == 0:
                    pe.wait_ge(h0_ready, NC_ * MT)
                with pe.Fori(0, NC_) as c:
                    for m in range(MT):
                        pe.wait_ge(act_tile, c * MT + (layer + 1) * (NC_ * MT) + m - MT + 1)
                        for k in range(MT):
                            ins = nc.tensor.matmul(ps[:, m, :], w[:, k, m * P:(m + 1) * P],
                                                   src[:, k, bass.ds(c * C, C)],
                                                   start=(k == 0), stop=(k == MT - 1))
                        ins.then_inc(gelu_mm, 1)

            pe.wait_ge(w3_ready, 1)
            for c in range(NC_):
                pe.wait_ge(act_tile, (2 * NC_ + c + 1) * MT)
                if c >= 2:
                    pe.wait_ge(z_ready, NC_ + c - 1)
                for t in range(TILES):
                    for k in range(MT):
                        ins = nc.tensor.matmul(ps[:, W3_BANK + c % 2, t * P:(t + 1) * P],
                                               hid[0][:, k, c * C + t * P:c * C + (t + 1) * P], w3_sb[:, k, :],
                                               start=(k == 0), stop=(k == MT - 1))
                ins.then_inc(w3_done, 1)


def kernel(L0_attn_x, L0_attn_wq, L0_attn_bq, L0_attn_wk, L0_attn_bk, L0_attn_wv, L0_attn_bv,
           L0_attn_wo, L0_attn_bo, L0_ffn_w1_w, L0_ffn_w1_s, L0_ffn_w2_w, L0_ffn_w2_s,
           L0_ffn_h1_w, L0_ffn_h1_s, L0_ffn_h2_w, L0_ffn_h2_s, L0_ffn_w3_w, L0_ffn_w3_s):
    import numpy as np
    import concourse.bacc as bacc
    from concourse.bass_utils import run_bass_kernel_spmd

    def columns(v, n):
        return np.ascontiguousarray(np.asarray(v).reshape(n, -1).T)

    def turned(w):
        return np.ascontiguousarray(np.asarray(w).T)

    x = np.ascontiguousarray(np.asarray(L0_attn_x).reshape(TOK, D))
    arrays = {
        "xT": turned(x), "x": x,
        "wqT": turned(L0_attn_wq), "wkT": turned(L0_attn_wk), "wvT": turned(L0_attn_wv),
        "woT": turned(L0_attn_wo),
        "bq": columns(L0_attn_bq, 1), "bk": columns(L0_attn_bk, 1),
        "bv": np.ascontiguousarray(L0_attn_bv), "bo": np.ascontiguousarray(L0_attn_bo),
        "w1T": turned(L0_ffn_w1_w), "w2T": turned(L0_ffn_w2_w),
        "h1T": turned(L0_ffn_h1_w), "h2T": turned(L0_ffn_h2_w), "w3T": turned(L0_ffn_w3_w),
        "w1s": columns(L0_ffn_w1_s, MT), "w2s": columns(L0_ffn_w2_s, MT),
        "h1s": columns(L0_ffn_h1_s, MT), "h2s": columns(L0_ffn_h2_s, MT),
        "w3s": np.ascontiguousarray(L0_ffn_w3_s),
    }
    nc = bacc.Bacc("TRN2", target_bir_lowering=False, num_devices=1)
    args = {n: nc.dram_tensor(f"in_{n}", a.shape, F32, kind="ExternalInput").ap() for n, a in arrays.items()}
    parts = {n: nc.dram_tensor(f"parts_{n}", (PARTS, DH, QC, G_ALL, HG, C), BF16, kind="Internal").ap()
             for n in "qk"}
    out = nc.dram_tensor("out", (TOK, D), F32, kind="ExternalOutput").ap()
    build(nc, parts_dram=parts, out=out, **args)
    r = run_bass_kernel_spmd(nc, [{f"in_{n}": a for n, a in arrays.items()}], core_ids=[0])
    return r.results[0]["out"].reshape(B, L, D)
```

```python
from contextlib import ExitStack

import concourse.bass as bass
from concourse import mybir

ALU = mybir.AluOpType
ACT = mybir.ActivationFunctionType
AX = mybir.AxisListType
F32 = mybir.dt.float32
BF16 = mybir.dt.bfloat16

P = 128
B, L, D = 2, 1024, 128
H, DH = 16, 8
HID = 512
TOK = B * L
SCALE = 1.0 / H ** 0.5
EPS = 1e-5

C = 512
NC_ = TOK // C
HG = 4
NG = H // HG
G_ALL = B * NG
QC = L // C
U_ALL = G_ALL * QC
KT = L // P
PARTS = 3
ROWS = DH * PARTS * PARTS
MROWS = ROWS + PARTS
QT = C // P
TURNS = HG * QT
LEAD = 6
TSTEP = 5
PER = 4
STEPS = PER * KT
ITERS = U_ALL // PER
LOAD_INC = 16 * 2 * PARTS
PARTS_INC = 16 * PARTS * (1 + QC)
MROW_INC = 16
MT = HID // P
TILES = C // P

ST_BANK, MAX_BANK, PV_BANK, T_BANK = 0, 2, 6, 7
JOB_BANKS = [0, 1, 6, 7]
WO_BANK, X1T_BANK, W3_BANK = 6, 7, 4

JOBS = [("k", 0), ("k", 1), ("q", 0), ("q", 1), ("k", 2), ("k", 3), ("q", 2), ("q", 3)]


def build(nc, xT, x, wqT, wkT, wvT, woT, bq, bk, bv, bo, w1T, w2T, h1T, h2T, w3T,
          w1s, w2s, h1s, h2s, w3s, k_dram, q_dram, den_dram, out):
    with ExitStack() as ctx:
        def sb(name, shape, dt=F32):
            return ctx.enter_context(nc.sbuf_tensor(name, shape, dt))

        def sem(name):
            return ctx.enter_context(nc.semaphore(name))

        xT_sb = sb("xT_sb", [P, TOK])
        xres = sb("xres", [P, TOK // P, D])
        wq_sb, wk_sb, wv_sb = (sb(f"w{n}_sb", [P, D]) for n in "qkv")
        wo_sb = sb("wo_sb", [P, NG, D])
        w1_sb, w2_sb = sb("w1_sb", [P, HID]), sb("w2_sb", [P, HID])
        h1_sb, h2_sb = sb("h1_sb", [P, MT, HID]), sb("h2_sb", [P, MT, HID])
        w3_sb = sb("w3_sb", [P, MT, D])
        bq_sb, bk_sb = sb("bq_sb", [P, 1]), sb("bk_sb", [P, 1])
        bv_bc, bo_bc, s3_bc = (sb(n, [P, D]) for n in ("bv_bc", "bo_bc", "s3_bc"))
        s_sb = {n: sb(f"{n}_sb", [P, MT]) for n in ("w1s", "w2s", "h1s", "h2s")}
        ident, ident_bf = sb("ident", [P, P]), sb("ident_bf", [P, P], BF16)

        qk = sb("qk", [P, 4 * HG * L], BF16)
        qx = qk[:, 0:2 * HG * L].rearrange("p (s c h t) -> p s c h t", s=2, c=QC, h=HG)
        kx = qk[:, 2 * HG * L:4 * HG * L].rearrange("p (s h t) -> p s h t", s=2, h=HG)
        attn = sb("attn", [P, U_ALL, C])
        hid = [qk[:, :].bitcast(F32).rearrange("p (m t) -> p m t", m=MT),
               attn[:, :, :].rearrange("p u c -> p (u c)").rearrange("p (m t) -> p m t", m=MT)]
        proj = sb("proj", [P, len(JOBS), C])
        prt = sb("prt", [P, 2 * PARTS * TOK], BF16)
        part = {n: prt[:, a * PARTS * TOK:(a + 1) * PARTS * TOK].rearrange("p (i t) -> p i t", i=PARTS)
                for a, n in enumerate("qk")}
        later = prt[:, :].bitcast(F32)
        den = [proj[:, :, :], later[:, 0:8 * C].rearrange("p (u c) -> p u c", c=C)]
        x1T = later[:, 8 * C:12 * C]
        den_c = [sb(f"den_c{n}", [P, 16 * k]) for n, k in enumerate((8, 6, 1, 1))]
        v_sb = sb("v_sb", [P, G_ALL, KT, HG * DH])
        v_pad = sb("v_pad", [P, 2, KT, HG, 32])
        probs = sb("probs", [P, 2, HG, C])
        negmax = sb("negmax", [P, 2, TURNS])
        zeros = sb("zeros", [P, TURNS])
        mrest = sb("mrest", [P, TURNS])
        mpart = sb("mpart", [P, 2, P // TURNS, TURNS], BF16)
        mT = sb("mT", [P, 2, P], BF16)
        x1 = sb("x1", [P, TOK // P, D])
        gate = sb("gate", [P, 2, C])
        z = sb("z", [P, 2, TILES, D])
        stats, mv = sb("stats", [P, TILES, 6]), sb("mv", [P, 2, TILES, 2])
        veps, rstd, power = sb("veps", [P, TILES]), sb("rstd", [P, 2, TILES]), sb("power", [P, TILES])
        ps = ctx.enter_context(nc.psum_tensor("ps", [P, 8, C], F32))
        ps_t = ps[:, T_BANK, :].bitcast(BF16)[:, 0:P]

        in_x = [sem(f"in_x{c}") for c in range(NC_)]
        in_k, in_q, in_v = sem("in_k"), sem("in_q"), sem("in_v")
        in_mid = sem("in_mid")
        in_ffn = sem("in_ffn")
        ones_set = sem("ones_set")
        ident_ready = sem("ident_ready")
        job_done = sem("job_done")
        v_proj = sem("v_proj")
        proj_ready = sem("proj_ready")
        split_act = sem("split_act")
        split_dve = sem("split_dve")
        split_pool = sem("split_pool")
        v_ready = sem("v_ready")
        parts_out = [sem(f"parts_out{b}") for b in range(B)]
        rows_in = [sem(f"rows_in{s}") for s in range(2)]
        v_staged = sem("v_staged")
        max_scores = sem("max_scores")
        max_taken = sem("max_taken")
        msplit_step = sem("msplit_step")
        max_split = sem("max_split")
        max_turned = sem("max_turned")
        max_copied = sem("max_copied")
        mrow_in = [sem(f"mrow_in{s}") for s in range(2)]
        scores = sem("scores")
        exp_done = sem("exp_done")
        pv_done = sem("pv_done")
        unit_out = sem("unit_out")
        den_set = [sem(f"den_set{b}") for b in range(B)]
        DEN = [(0, 0, 8), (1, 0, 6), (1, 6, 7), (1, 7, 8)]
        den_in = [sem(f"den_in{n}") for n in range(len(DEN))]
        den_ready = sem("den_ready")
        den_out = sem("den_out")
        den_back = [sem(f"den_back{n}") for n in range(len(DEN))]
        xres_ready = sem("xres_ready")
        w3_ready = sem("w3_ready")
        chunk_normed = sem("chunk_normed")
        wo_done = sem("wo_done")
        z_ready = sem("z_ready")
        stats_ready = sem("stats_ready")
        var_ready = sem("var_ready")
        pow_step = sem("pow_step")
        rstd_ready = sem("rstd_ready")
        x1_ready = sem("x1_ready")
        x1_turned = sem("x1_turned")
        x1T_ready = sem("x1T_ready")
        gate_mm = sem("gate_mm")
        act_tile = sem("act_tile")
        h0_ready = sem("h0_ready")
        gelu_mm = sem("gelu_mm")
        w3_done = sem("w3_done")
        out_ready = sem("out_ready")
        out_in = sem("out_in")

        block = ctx.enter_context(nc.Block())

        @block.sync
        def _(sp):
            xT_c = xT.rearrange("p (c t) -> c p t", c=NC_)
            sp.dma_start(wk_sb[:], wkT).then_inc(in_k, 16)
            sp.dma_start(bk_sb[:], bk).then_inc(in_k, 16)
            sp.dma_start(xT_sb[:, 0:C], xT_c[0]).then_inc(in_x[0], 16)
            sp.dma_start(wq_sb[:], wqT).then_inc(in_q, 16)
            sp.dma_start(bq_sb[:], bq).then_inc(in_q, 16)
            for c in range(2, NC_):
                sp.dma_start(xT_sb[:, c * C:(c + 1) * C], xT_c[c]).then_inc(in_x[c], 16)
            sp.dma_start(wv_sb[:], wvT).then_inc(in_v, 16)
            sp.dma_start(bv_bc[:], bv.partition_broadcast(P)).then_inc(in_v, 16)

            def store_k(b):
                for i in range(PARTS):
                    sp.dma_start(k_dram[i, :, b * NG:(b + 1) * NG].rearrange("d g h t -> (g h) d t"),
                                 part["k"][:, i, b * L:(b + 1) * L]).then_inc(parts_out[b], 16)

            def store_q(c):
                b, qc = c // QC, c % QC
                for i in range(PARTS):
                    sp.dma_start(q_dram[i, :, qc, b * NG:(b + 1) * NG].rearrange("d g h t -> (g h) d t"),
                                 part["q"][:, i, c * C:(c + 1) * C]).then_inc(parts_out[b], 16)

            def load_rows(g, slot):
                for j in range(PARTS):
                    r = slice(DH * PARTS * j, DH * PARTS * (j + 1))
                    src = k_dram[j, :, bass.ds(g, 1)].rearrange("d o h t -> o d (h t)")
                    sp.dma_start(kx[r, slot].rearrange("r h t -> r (h t)"),
                                 src.broadcast_to([PARTS, DH, HG * L]))\
                      .then_inc(rows_in[slot], 16)
                for j in range(PARTS):
                    r = slice(DH * PARTS * j, DH * PARTS * (j + 1))
                    src = q_dram[:, :, :, bass.ds(g, 1)].rearrange("i d c o h t -> (i d) c (o h t)")
                    sp.dma_start(qx[r, slot].rearrange("r c h t -> r c (h t)"), src)\
                      .then_inc(rows_in[slot], 16)

            def load_max(i, w):
                slot, qc = w // QC % 2, w % QC
                sp.wait_ge(max_copied, i * PER + w + 1)
                sp.dma_start(qx[ROWS:MROWS, slot, qc, :, :].rearrange("i h t -> i (h t)"),
                             mT[0:PARTS * TURNS, w % 2, :]).then_inc(mrow_in[w % 2], 16)

            sp.wait_ge(ones_set, 1)
            sp.wait_ge(split_dve, 2 * 4)
            store_k(0)
            for c in range(QC):
                sp.wait_ge(split_dve, (3 + c) * 4)
                store_q(c)
            sp.wait_ge(parts_out[0], PARTS_INC)
            load_rows(0, 0)
            load_rows(1, 1)
            load_max(0, 0)
            sp.wait_ge(split_pool, 2 * 3)
            store_k(1)
            for c in range(QC):
                sp.wait_ge(split_pool, (3 + c) * 3)
                store_q(QC + c)
            sp.wait_ge(parts_out[1], PARTS_INC)

            def units(i, last):
                load_max(i, 1)
                load_max(i, 2)
                if not last:
                    sp.wait_ge(scores, i * (STEPS * HG) + STEPS * HG // 2)
                    load_rows(i * 2 + 2, 0)
                load_max(i, 3)
                if not last:
                    load_max(i, 4)
                    sp.wait_ge(scores, i * (STEPS * HG) + STEPS * HG)
                    load_rows(i * 2 + 3, 1)

            with sp.Fori(0, ITERS - 1) as i:
                units(i, False)
            for n, dst, src in ((in_ffn, w1_sb[:], w1T), (in_ffn, w2_sb[:], w2T),
                                (in_ffn, h1_sb[:], h1T.rearrange("(k p) o -> p k o", p=P)),
                                (in_ffn, h2_sb[:], h2T.rearrange("(k p) o -> p k o", p=P)),
                                (in_ffn, w3_sb[:], w3T.rearrange("(k p) o -> p k o", p=P)),
                                (in_ffn, s3_bc[:], w3s.partition_broadcast(P)),
                                (in_ffn, s_sb["w1s"][:], w1s), (in_ffn, s_sb["w2s"][:], w2s),
                                (in_ffn, s_sb["h1s"][:], h1s), (in_ffn, s_sb["h2s"][:], h2s)):
                sp.dma_start(dst, src).then_inc(n, 16)
            units(ITERS - 1, True)
            def gather(n):
                b, u0, u1 = DEN[n]
                sp.wait_ge(unit_out, b * 8 + u1)
                for j in range(HG):
                    row = attn[32 * j + DH:32 * j + DH + 1, b * 8 + u0:b * 8 + u1, :]
                    sp.dma_start(den_c[n][32 * j:32 * j + 32, :],
                                 row.rearrange("o u c -> o (u c)").rearrange("o (x y) -> o x y", x=32))\
                      .then_inc(den_in[n], 16)

            def spread(n):
                b, u0, u1 = DEN[n]
                sp.wait_ge(den_ready, n + 1)
                dram = den_dram[:, (b * 8 + u0) * C:(b * 8 + u1) * C]
                sp.dma_start(dram.rearrange("j (x y) -> j x y", x=32), den_c[n][:, :]).then_inc(den_out, 16)
                sp.wait_ge(den_out, 16 * n + 16)
                sp.wait_ge(den_set[b], 1)
                for j in range(HG):
                    sp.dma_start(den[b][32 * j:32 * j + DH, u0:u1, :].rearrange("p u c -> p (u c)"),
                                 dram[j].partition_broadcast(DH)).then_inc(den_back[n], 16)

            gather(0)
            spread(0)
            gather(1)
            spread(1)
            gather(2)
            gather(3)
            spread(2)
            spread(3)
            out_c = out.rearrange("(c t p) d -> c p t d", p=P, t=TILES)
            for c in range(NC_):
                sp.wait_ge(out_ready, c + 1)
                sp.dma_start(out_c[c], xres[:, c * TILES:(c + 1) * TILES, :]).then_inc(out_in, 16)
            sp.wait_ge(out_in, 16 * NC_)

        @block.scalar
        def _(act):
            xT_c = xT.rearrange("p (c t) -> c p t", c=NC_)
            act.dma_start(xT_sb[:, C:2 * C], xT_c[1]).then_inc(in_x[1], 16)
            act.dma_start(xres[:], x.rearrange("(t p) d -> p t d", p=P)).then_inc(in_mid, 16)
            act.dma_start(bo_bc[:], bo.partition_broadcast(P)).then_inc(in_mid, 16)
            act.wait_ge(ones_set, 2)
            for j in range(HG):
                act.dma_start(wo_sb[32 * j:32 * j + DH, :, :],
                              woT.rearrange("(g j d) e -> j d g e", g=NG, j=HG)[j]).then_inc(in_mid, 16)
            act.wait_ge(in_k, 32)
            act.wait_ge(in_q, 32)
            for n, (name, c) in enumerate(JOBS):
                act.wait_ge(job_done, n + 1)
                nc.scalar.activation(proj[:, n, :], ps[:, JOB_BANKS[n % 4], :], ACT.Identity,
                                     bias=(bq_sb if name == "q" else bk_sb)[:, 0:1]).then_inc(proj_ready, 1)
                act.wait_ge(proj_ready, n + 1)
                if n >= 4:
                    nc.scalar.activation(part[name][:, 0, c * C:(c + 1) * C], proj[:, n, :],
                                         ACT.Copy).then_inc(split_act, 1)

            def exps(i, k, heads=range(HG)):
                for h in heads:
                    act.wait_ge(scores, i * (STEPS * HG) + k * HG + h + 1)
                    nc.scalar.activation(probs[:, k % 2, h, :], ps[:, ST_BANK + h % 2, :], ACT.Exp,
                                         scale=SCALE).then_inc(exp_done, 1)

            attn_flat = attn[:, :, :].rearrange("p u c -> p (u c)")

            def units(i, last):
                for k in range(STEPS):
                    if not (last and k == STEPS - 1):
                        exps(i, k + 1, (0, 1))
                    if k % KT == KT - 1:
                        act.wait_ge(pv_done, i * STEPS + k + 1)
                        nc.scalar.activation(attn_flat[:, bass.ds(i * (PER * C) + k // KT * C, C)],
                                             ps[:, PV_BANK, :], ACT.Copy).then_inc(unit_out, 1)
                    if not (last and k == STEPS - 1):
                        exps(i, k + 1, (2, 3))

            exps(0, 0)
            with act.Fori(0, ITERS - 1) as i:
                units(i, False)
            units(ITERS - 1, True)

            act.wait_ge(in_ffn, 160)
            for c in range(NC_):
                act.wait_ge(x1_turned, c + 1)
                nc.scalar.activation(x1T[:, c * C:(c + 1) * C], ps[:, X1T_BANK, :], ACT.Copy)\
                  .then_inc(x1T_ready, 1)
                for m in range(MT):
                    n = c * MT + m
                    act.wait_ge(gate_mm, n + 1)
                    if n >= 2:
                        act.wait_ge(h0_ready, n - 1)
                    nc.scalar.activation(gate[:, n % 2, :], ps[:, 2 * (n % 2), :], ACT.Silu,
                                         scale=s_sb["w1s"][:, m:m + 1]).then_inc(act_tile, 1)
            for layer, scale in enumerate(("h1s", "h2s")):
                dst = hid[1 - layer]

                def chunk(c):
                    for m in range(MT):
                        act.wait_ge(gelu_mm, c * MT + layer * (NC_ * MT) + m + 1)
                        nc.scalar.activation(dst[:, m, bass.ds(c * C, C)], ps[:, m, :], ACT.Gelu,
                                             scale=s_sb[scale][:, m:m + 1]).then_inc(act_tile, 1)

                with act.Fori(0, NC_) as c:
                    chunk(c)

        @block.gpsimd
        def _(pool):
            nc.gpsimd.memset(kx[64:MROWS, :, :, :], 1.0).then_inc(ones_set, 1)
            pool.wait_ge(ones_set, 1)
            nc.gpsimd.memset(wo_sb[:], 0.0).then_inc(ones_set, 1)
            nc.gpsimd.memset(ident[:], 1.0).then_inc(ident_ready, 1)
            pool.wait_ge(ident_ready, 1)
            nc.gpsimd.affine_select(out=ident[:], in_=ident[:], compare_op=ALU.is_equal, fill=0.0, base=0,
                                    pattern=[[-1, P]], channel_multiplier=1).then_inc(ident_ready, 1)
            pool.wait_ge(ident_ready, 2)
            nc.gpsimd.tensor_copy(ident_bf[:], ident[:]).then_inc(ident_ready, 1)
            nc.gpsimd.memset(power[:], -0.5).then_inc(ones_set, 1)
            nc.gpsimd.memset(v_pad[:], 1.0).then_inc(ones_set, 1)
            nc.gpsimd.memset(mpart[:], 0.0).then_inc(ones_set, 1)
            nc.gpsimd.memset(zeros[:], 0.0).then_inc(ones_set, 1)
            pool.wait_ge(ones_set, 6)

            def stage_v(g, slot):
                nc.gpsimd.tensor_copy(
                    v_pad[:, slot, :, :, 0:DH],
                    v_sb[:, :, :, :].rearrange("p g k (h d) -> p (g k) h d", h=HG)[:, bass.ds(g * KT, KT), :, :]
                ).then_inc(v_staged, 1)

            def split(n):
                name, c = JOBS[n]
                at = slice(c * C, (c + 1) * C)
                done = 3 * (n - 4)
                pool.wait_ge(split_act, n - 3)
                nc.gpsimd.tensor_tensor(proj[:, n, :], proj[:, n, :], part[name][:, 0, at],
                                        ALU.subtract).then_inc(split_pool, 1)
                pool.wait_ge(split_pool, done + 1)
                nc.gpsimd.tensor_copy(part[name][:, 1, at], proj[:, n, :]).then_inc(split_pool, 1)
                pool.wait_ge(split_pool, done + 2)
                nc.gpsimd.tensor_tensor(part[name][:, 2, at], proj[:, n, :], part[name][:, 1, at],
                                        ALU.subtract).then_inc(split_pool, 1)

            def split_max(i, w):
                m, parts = negmax[:, w % 2, :], mpart[:, w % 2, :, :]
                done = i * (3 * PER) + 3 * w
                pool.wait_ge(max_taken, i * (PER * TURNS) + w * TURNS + TURNS)
                nc.gpsimd.tensor_tensor(parts[:, 0, :], m, zeros[:], ALU.add).then_inc(msplit_step, 1)
                pool.wait_ge(msplit_step, done + 1)
                nc.gpsimd.tensor_tensor(mrest[:], m, parts[:, 0, :], ALU.subtract).then_inc(msplit_step, 1)
                pool.wait_ge(msplit_step, done + 2)
                nc.gpsimd.tensor_tensor(parts[:, 1, :], mrest[:], zeros[:], ALU.add)\
                  .then_inc(msplit_step, 1)
                pool.wait_ge(msplit_step, done + 3)
                nc.gpsimd.tensor_tensor(parts[:, 2, :], mrest[:], parts[:, 1, :], ALU.subtract)\
                  .then_inc(max_split, 1)

            split(4)
            split(5)
            pool.wait_ge(v_ready, 2)
            stage_v(0, 0)
            stage_v(1, 1)
            split_max(0, 0)
            split(6)
            split(7)
            pool.wait_ge(v_ready, NC_)

            def units(i, last):
                split_max(i, 1)
                split_max(i, 2)
                if not last:
                    pool.wait_ge(pv_done, i * STEPS + STEPS // 2)
                    stage_v(i * 2 + 2, 0)
                split_max(i, 3)
                if not last:
                    split_max(i, 4)
                    pool.wait_ge(pv_done, i * STEPS + STEPS)
                    stage_v(i * 2 + 3, 1)

            with pool.Fori(0, ITERS - 1) as i:
                units(i, False)
            pool.wait_ge(split_dve, 4 * 4)
            pool.wait_ge(split_pool, 3 * 4)
            for b in range(B):
                pool.wait_ge(parts_out[b], PARTS_INC)
            for b in range(B):
                nc.gpsimd.memset(den[b], 1.0).then_inc(den_set[b], 1)
            pool.wait_ge(in_mid, 96)
            nc.gpsimd.tensor_tensor(xres[:], xres[:], bo_bc[:, :].unsqueeze(1).broadcast_to([P, TOK // P, D]),
                                    ALU.add).then_inc(xres_ready, 1)
            pool.wait_ge(in_ffn, 160)
            nc.gpsimd.tensor_tensor(w3_sb[:], w3_sb[:], s3_bc[:, :].unsqueeze(1).broadcast_to([P, MT, D]),
                                    ALU.mult).then_inc(w3_ready, 1)
            units(ITERS - 1, True)
            for n in range(2 * NC_):
                pool.wait_ge(var_ready, n + 1)
                nc.gpsimd.tensor_scalar(veps[:], mv[:, n % 2, :, 1], EPS, None, ALU.add).then_inc(pow_step, 1)
                pool.wait_ge(pow_step, n + 1)
                nc.gpsimd.tensor_tensor(rstd[:, n % 2, :], veps[:], power[:], ALU.pow).then_inc(rstd_ready, 1)

        @block.vector
        def _(dve):
            def split(n):
                name, c = JOBS[n]
                at = slice(c * C, (c + 1) * C)
                done = 4 * n
                dve.wait_ge(proj_ready, n + 1)
                nc.vector.tensor_copy(part[name][:, 0, at], proj[:, n, :]).then_inc(split_dve, 1)
                dve.wait_ge(split_dve, done + 1)
                nc.vector.tensor_tensor(proj[:, n, :], proj[:, n, :], part[name][:, 0, at],
                                        ALU.subtract).then_inc(split_dve, 1)
                dve.wait_ge(split_dve, done + 2)
                nc.vector.tensor_copy(part[name][:, 1, at], proj[:, n, :]).then_inc(split_dve, 1)
                dve.wait_ge(split_dve, done + 3)
                nc.vector.tensor_tensor(part[name][:, 2, at], proj[:, n, :], part[name][:, 1, at],
                                        ALU.subtract).then_inc(split_dve, 1)

            for n in range(4):
                split(n)
            dve.wait_ge(in_v, 32)
            for c in range(NC_):
                dve.wait_ge(v_proj, c + 1)
                b, k0 = c // (NC_ // B), (c % (NC_ // B)) * TILES
                nc.vector.tensor_tensor(
                    v_sb[:, b * NG:(b + 1) * NG, k0:k0 + TILES, :],
                    ps[:, MAX_BANK + c, :].rearrange("p (t g e) -> p g t e", t=TILES, g=NG),
                    bv_bc[:, :].rearrange("p (g e) -> p g e", g=NG).unsqueeze(2)
                    .broadcast_to([P, NG, TILES, HG * DH]),
                    ALU.add).then_inc(v_ready, 1)

            def turn(i, t):
                dve.wait_ge(max_scores, i * (PER * TURNS) + t + 1)
                if t % TURNS == 0 and t >= 2 * TURNS:
                    dve.wait_ge(max_split, i * PER + t // TURNS - 1)
                bank = MAX_BANK + 2 * (t % 2)
                nc.vector.tensor_reduce(negmax[:, t // TURNS % 2, t % TURNS:t % TURNS + 1],
                                        ps[:, bank:bank + 2, :], AX.XY, ALU.max, negate=True)\
                  .then_inc(max_taken, 1)

            def copy_max(i, w):
                dve.wait_ge(max_turned, i * PER + w + 1)
                nc.vector.tensor_copy(mT[:, w % 2, :], ps_t).then_inc(max_copied, 1)

            for t in range(TURNS + LEAD):
                turn(0, t)
            copy_max(0, 0)

            def units(i, last):
                for k in range(STEPS):
                    for t in (TURNS + LEAD + 2 * k, TURNS + LEAD + 2 * k + 1):
                        if not (last and t >= PER * TURNS):
                            turn(i, t)
                    if k % KT == TSTEP and not (last and k // KT == PER - 1):
                        copy_max(i, k // KT + 1)

            with dve.Fori(0, ITERS - 1) as i:
                units(i, False)
            units(ITERS - 1, True)

            def invert(n):
                dve.wait_ge(den_in[n], 64)
                nc.vector.reciprocal(den_c[n][:], den_c[n][:]).then_inc(den_ready, 1)

            def norm(c):
                b, qc = c // QC, c % QC
                if c == 0:
                    dve.wait_ge(den_back[0], 64)
                if c == QC:
                    dve.wait_ge(den_back[1], 64)
                for g in range(NG):
                    u = g * QC + qc
                    if b == B - 1 and g == NG - 1:
                        dve.wait_ge(den_back[2 + qc], 64)
                    ins = nc.vector.tensor_tensor(attn[:, b * 8 + u, :], attn[:, b * 8 + u, :],
                                                  den[b][:, u, :], ALU.mult)
                ins.then_inc(chunk_normed, 1)

            def layernorm(n, psum, add, dst):
                zc, st, m = z[:, n % 2], stats, mv[:, n % 2]
                nc.vector.tensor_tensor(zc, psum.rearrange("p (t d) -> p t d", t=TILES), add, ALU.add)\
                  .then_inc(z_ready, 1)
                dve.wait_ge(z_ready, n + 1)
                for t in range(TILES):
                    ins = nc.vector.bn_stats(st[:, t, :], zc[:, t, :])
                ins.then_inc(stats_ready, 1)
                dve.wait_ge(stats_ready, n + 1)
                for t in range(TILES):
                    ins = nc.vector.bn_aggr(m[:, t, :], st[:, t, :])
                ins.then_inc(var_ready, 1)
                dve.wait_ge(rstd_ready, n + 1)
                for t in range(TILES):
                    ins = nc.vector.tensor_scalar(dst[:, t, :], zc[:, t, :], m[:, t, 0:1],
                                                  rstd[:, n % 2, t:t + 1], ALU.subtract, ALU.mult)
                return ins

            def gated(c):
                for m in range(MT):
                    n = c * MT + m
                    dve.wait_ge(act_tile, n + 1)
                    nc.vector.scalar_tensor_tensor(out=hid[0][:, m, c * C:(c + 1) * C],
                                                   in0=ps[:, 2 * (n % 2) + 1, :], scalar=s_sb["w2s"][:, m:m + 1],
                                                   in1=gate[:, n % 2, :], op0=ALU.mult, op1=ALU.mult)\
                      .then_inc(h0_ready, 1)

            def first(c):
                dve.wait_ge(wo_done, c + 1)
                if c == 0:
                    dve.wait_ge(xres_ready, 1)
                at = slice(c * TILES, (c + 1) * TILES)
                layernorm(c, ps[:, WO_BANK, :], xres[:, at, :], x1[:, at, :]).then_inc(x1_ready, 1)

            invert(0)
            norm(0)
            norm(1)
            invert(1)
            invert(2)
            invert(3)
            first(0)
            dve.wait_ge(in_ffn, 160)
            for c in range(1, NC_):
                if c + 1 < NC_:
                    norm(c + 1)
                first(c)
                gated(c - 1)
            gated(NC_ - 1)
            for c in range(NC_):
                dve.wait_ge(w3_done, c + 1)
                at = slice(c * TILES, (c + 1) * TILES)
                layernorm(NC_ + c, ps[:, W3_BANK + c % 2, :], x1[:, at, :], xres[:, at, :])\
                  .then_inc(out_ready, 1)

        @block.tensor
        def _(pe):
            for n, (name, c) in enumerate(JOBS):
                pe.wait_ge(in_x[c], 16)
                if n == 0:
                    pe.wait_ge(in_k, 32)
                if n == 2:
                    pe.wait_ge(in_q, 32)
                if n >= 4:
                    pe.wait_ge(proj_ready, n - 3)
                nc.tensor.matmul(ps[:, JOB_BANKS[n % 4], :], (wq_sb if name == "q" else wk_sb)[:],
                                 xT_sb[:, c * C:(c + 1) * C], start=True, stop=True).then_inc(job_done, 1)
                if n == 3:
                    pe.wait_ge(in_v, 32)
                    for c in range(NC_):
                        pe.wait_ge(in_x[c], 16)
                        for t in range(TILES):
                            ins = nc.tensor.matmul(ps[:, MAX_BANK + c, t * P:(t + 1) * P],
                                                   xT_sb[:, c * C + t * P:c * C + (t + 1) * P], wv_sb[:],
                                                   start=True, stop=True)
                        ins.then_inc(v_proj, 1)

            def turn(i, t, half):
                slot, qc, h, q = t // (QC * TURNS) % 2, t // TURNS % QC, t % TURNS // QT, t % QT
                if half == 0:
                    if t >= 2:
                        pe.wait_ge(max_taken, i * (PER * TURNS) + t - 1)
                    if t % (QC * TURNS) == 0:
                        pe.wait_ge(rows_in[slot], i * LOAD_INC + (t // (PER * TURNS) + 1) * LOAD_INC)
                ins = nc.tensor.matmul(ps[:, MAX_BANK + 2 * (t % 2) + half, :],
                                       qx[0:ROWS, slot, qc, h, q * P:(q + 1) * P],
                                       kx[0:ROWS, slot, h, half * C:(half + 1) * C], start=True, stop=True)
                if half == 1:
                    ins.then_inc(max_scores, 1)

            def turn_max(i, w):
                pe.wait_ge(max_split, i * PER + w + 1)
                pe.wait_ge(max_copied, i * PER + w)
                nc.tensor.transpose(ps_t, mpart[:, w % 2, :, :].rearrange("p i t -> p (i t)"), ident_bf[:])\
                  .then_inc(max_turned, 1)

            def score(i, k, h):
                w, kt = k // KT, k % KT
                slot, qc = w // QC % 2, w % QC
                if k > 0 or h >= 2:
                    pe.wait_ge(exp_done, i * (STEPS * HG) + k * HG + h - 1)
                if kt == 0 and h == 0:
                    pe.wait_ge(mrow_in[w % 2], i * (PER // 2 * MROW_INC) + (w // 2 + 1) * MROW_INC)
                nc.tensor.matmul(ps[:, ST_BANK + h % 2, :], kx[0:MROWS, slot, h, kt * P:(kt + 1) * P],
                                 qx[0:MROWS, slot, qc, h, :], start=True, stop=True)\
                  .then_inc(scores, 1)

            def product(i, k):
                w, kt = k // KT, k % KT
                if kt == 0 and w % QC == 0:
                    pe.wait_ge(v_staged, i * (PER // QC) + w // QC + 1)
                pe.wait_ge(exp_done, i * (STEPS * HG) + k * HG + HG)
                for h in range(HG):
                    ins = nc.tensor.matmul(ps[32 * h:32 * h + 32, PV_BANK, :], v_pad[:, w // QC, kt, h, :],
                                           probs[:, k % 2, h, :], start=(kt == 0), stop=(kt == KT - 1),
                                           tile_position=(0, 32 * h))
                ins.then_inc(pv_done, 1)

            pe.wait_ge(v_ready, NC_)
            for t in range(TURNS + LEAD):
                turn(0, t, 0)
                turn(0, t, 1)
            pe.wait_ge(proj_ready, len(JOBS))
            pe.wait_ge(ident_ready, 3)
            turn_max(0, 0)
            for h in range(HG):
                score(0, 0, h)

            def units(i, last):
                for k in range(STEPS):
                    more = not (last and k == STEPS - 1)
                    t = TURNS + LEAD + 2 * k
                    turns = not (last and t >= PER * TURNS)
                    if more:
                        score(i, k + 1, 0)
                        score(i, k + 1, 1)
                    product(i, k)
                    if turns:
                        turn(i, t, 0)
                    if more:
                        score(i, k + 1, 2)
                    if turns:
                        turn(i, t, 1)
                    if more:
                        score(i, k + 1, 3)
                    if turns:
                        turn(i, t + 1, 0)
                        turn(i, t + 1, 1)
                    if k % KT == TSTEP and not (last and k // KT == PER - 1):
                        turn_max(i, k // KT + 1)

            with pe.Fori(0, ITERS - 1) as i:
                units(i, False)
            units(ITERS - 1, True)

            def out_proj(c):
                b, qc = c // QC, c % QC
                pe.wait_ge(chunk_normed, c + 1)
                if c == 0:
                    pe.wait_ge(in_mid, 96)
                    pe.wait_ge(unit_out, U_ALL)
                if c >= 1:
                    pe.wait_ge(z_ready, c)
                for t in range(TILES):
                    for g in range(NG):
                        ins = nc.tensor.matmul(ps[:, WO_BANK, t * P:(t + 1) * P],
                                               attn[:, b * 8 + g * QC + qc, t * P:(t + 1) * P], wo_sb[:, g, :],
                                               start=(g == 0), stop=(g == NG - 1))
                ins.then_inc(wo_done, 1)

            def turn_x1(c):
                pe.wait_ge(x1_ready, c + 1)
                if c >= 1:
                    pe.wait_ge(x1T_ready, c)
                for t in range(TILES):
                    ins = nc.tensor.transpose(ps[:, X1T_BANK, t * P:(t + 1) * P], x1[:, c * TILES + t, :],
                                              ident[:])
                ins.then_inc(x1_turned, 1)

            def gate_products(c):
                if c == 0:
                    pe.wait_ge(in_ffn, 160)
                pe.wait_ge(x1T_ready, c + 1)
                for m in range(MT):
                    n = c * MT + m
                    if n >= 2:
                        pe.wait_ge(h0_ready, n - 1)
                    for a, w in enumerate((w1_sb, w2_sb)):
                        ins = nc.tensor.matmul(ps[:, 2 * (n % 2) + a, :], w[:, m * P:(m + 1) * P],
                                               x1T[:, c * C:(c + 1) * C], start=True, stop=True)
                    ins.then_inc(gate_mm, 1)

            out_proj(0)
            out_proj(1)
            turn_x1(0)
            gate_products(0)
            for c in range(1, NC_):
                if c + 1 < NC_:
                    out_proj(c + 1)
                turn_x1(c)
                gate_products(c)

            for layer, w in enumerate((h1_sb, h2_sb)):
                src = hid[layer]
                if layer == 0:
                    pe.wait_ge(h0_ready, NC_ * MT)
                with pe.Fori(0, NC_) as c:
                    for m in range(MT):
                        pe.wait_ge(act_tile, c * MT + (layer + 1) * (NC_ * MT) + m - MT + 1)
                        for k in range(MT):
                            ins = nc.tensor.matmul(ps[:, m, :], w[:, k, m * P:(m + 1) * P],
                                                   src[:, k, bass.ds(c * C, C)],
                                                   start=(k == 0), stop=(k == MT - 1))
                        ins.then_inc(gelu_mm, 1)

            pe.wait_ge(w3_ready, 1)
            for c in range(NC_):
                pe.wait_ge(act_tile, (2 * NC_ + c + 1) * MT)
                if c >= 2:
                    pe.wait_ge(z_ready, NC_ + c - 1)
                for t in range(TILES):
                    for k in range(MT):
                        ins = nc.tensor.matmul(ps[:, W3_BANK + c % 2, t * P:(t + 1) * P],
                                               hid[0][:, k, c * C + t * P:c * C + (t + 1) * P], w3_sb[:, k, :],
                                               start=(k == 0), stop=(k == MT - 1))
                ins.then_inc(w3_done, 1)


def kernel(L0_attn_x, L0_attn_wq, L0_attn_bq, L0_attn_wk, L0_attn_bk, L0_attn_wv, L0_attn_bv,
           L0_attn_wo, L0_attn_bo, L0_ffn_w1_w, L0_ffn_w1_s, L0_ffn_w2_w, L0_ffn_w2_s,
           L0_ffn_h1_w, L0_ffn_h1_s, L0_ffn_h2_w, L0_ffn_h2_s, L0_ffn_w3_w, L0_ffn_w3_s):
    import numpy as np
    import concourse.bacc as bacc
    from concourse.bass_utils import run_bass_kernel_spmd

    def columns(v, n):
        return np.ascontiguousarray(np.asarray(v).reshape(n, -1).T)

    def turned(w):
        return np.ascontiguousarray(np.asarray(w).T)

    x = np.ascontiguousarray(np.asarray(L0_attn_x).reshape(TOK, D))
    arrays = {
        "xT": turned(x), "x": x,
        "wqT": turned(L0_attn_wq), "wkT": turned(L0_attn_wk), "wvT": turned(L0_attn_wv),
        "woT": turned(L0_attn_wo),
        "bq": columns(L0_attn_bq, 1), "bk": columns(L0_attn_bk, 1),
        "bv": np.ascontiguousarray(L0_attn_bv), "bo": np.ascontiguousarray(L0_attn_bo),
        "w1T": turned(L0_ffn_w1_w), "w2T": turned(L0_ffn_w2_w),
        "h1T": turned(L0_ffn_h1_w), "h2T": turned(L0_ffn_h2_w), "w3T": turned(L0_ffn_w3_w),
        "w1s": columns(L0_ffn_w1_s, MT), "w2s": columns(L0_ffn_w2_s, MT),
        "h1s": columns(L0_ffn_h1_s, MT), "h2s": columns(L0_ffn_h2_s, MT),
        "w3s": np.ascontiguousarray(L0_ffn_w3_s),
    }
    nc = bacc.Bacc("TRN2", target_bir_lowering=False, num_devices=1)
    args = {n: nc.dram_tensor(f"in_{n}", a.shape, F32, kind="ExternalInput").ap() for n, a in arrays.items()}
    k_dram = nc.dram_tensor("parts_k", (PARTS, DH, G_ALL, HG, L), BF16, kind="Internal").ap()
    q_dram = nc.dram_tensor("parts_q", (PARTS, DH, QC, G_ALL, HG, C), BF16, kind="Internal").ap()
    den_dram = nc.dram_tensor("den", (HG, U_ALL * C), F32, kind="Internal").ap()
    out = nc.dram_tensor("out", (TOK, D), F32, kind="ExternalOutput").ap()
    build(nc, k_dram=k_dram, q_dram=q_dram, den_dram=den_dram, out=out, **args)
    r = run_bass_kernel_spmd(nc, [{f"in_{n}": a for n, a in arrays.items()}], core_ids=[0])
    return r.results[0]["out"].reshape(B, L, D)
```

```python
from contextlib import ExitStack

import concourse.bass as bass
from concourse import mybir

ALU = mybir.AluOpType
ACT = mybir.ActivationFunctionType
AX = mybir.AxisListType
F32 = mybir.dt.float32
BF16 = mybir.dt.bfloat16

P = 128
B, L, D = 2, 1024, 128
H, DH = 16, 8
HID = 512
TOK = B * L
SCALE = 1.0 / H ** 0.5
EPS = 1e-5

C = 512
NC_ = TOK // C
HG = 4
NG = H // HG
G_ALL = B * NG
QC = L // C
U_ALL = G_ALL * QC
KT = L // P
PARTS = 3
ROWS = DH * PARTS * PARTS
MROWS = ROWS + PARTS
QT = C // P
TURNS = HG * QT
LEAD = 7
TSTEP = 5
PER = 4
STEPS = PER * KT
ITERS = U_ALL // PER
LOAD_INC = [16 * (PARTS + 1), 16 * PARTS]
STORE_INC = 16 * PARTS
MROW_INC = 16
MT = HID // P
TILES = C // P

ST_BANK = [0, 1, 7, 1]
MAX_BANK, PV_BANK, T_BANK = 2, 6, 7
JOB_BANKS = [0, 1, 6, 7]
WO_BANK, X1T_BANK, INEXACT_BANK = [2, 3, 6, 7], [5, 4, 6, 7], 4
GATE_BANK, GELU_BANK, W3_BANK = 0, 4, 0
SLICE = {"w1": 0, "w2": 1, "h1": 2, "h2": 2 + MT, "w3": 2 + 2 * MT}
SLICES = 3 + 2 * MT
WINDOWS = (2, 3, 4, 2)
FLAGGED = 8
ORDER = [("gate", 0), ("gate", 1), ("h1", 0), ("h1", 1), ("gate", 2), ("gate", 3)]
ORDER += [("h1", c) for c in (2, 3)] + [("h2", c) for c in range(NC_)]
RING = 4
MOVES = [(0, 0, 8), (1, 0, 6), (1, 6, 7), (1, 7, 8)]
MOVED = [16 * HG * NG, 16 * HG * (NG - 1), 16 * HG, 16 * HG]
PIECES = [(3, 0, 2), (3, 2, 4)]

DVE_JOBS = [0, 1, 3]
JOBS = [("k", 0), ("k", 1), ("q", 0), ("q", 1), ("k", 2), ("k", 3), ("q", 2), ("q", 3)]


def build(nc, xT, x, wqT, wkT, wvT, woT, bq, bk, bv, bo, w1T, w2T, h1T, h2T, w3T,
          w1s, w2s, h1s, h2s, w3s, k_dram, q_dram, den_dram, out):
    with ExitStack() as ctx:
        def sb(name, shape, dt=F32):
            return ctx.enter_context(nc.sbuf_tensor(name, shape, dt))

        def sem(name):
            return ctx.enter_context(nc.semaphore(name))

        xT_sb = sb("xT_sb", [P, TOK])
        xres = sb("xres", [P, TOK // P, D])
        wq_sb, wk_sb, wv_sb = (sb(f"w{n}_sb", [P, D]) for n in "qkv")
        wo_sb = wq_sb
        w_sb = sb("w_sb", [P, SLICES, HID])
        w_first = sb("w_first", [P, SLICES, HID], BF16)
        w_more = w_sb[:, :, :].rearrange("p n c -> p (n c)").bitcast(BF16)\
            .rearrange("p (n a c) -> p n a c", a=2, c=HID)
        w_left = sb("w_left", [P, HID])
        bq_sb, bk_sb = sb("bq_sb", [P, 1]), sb("bk_sb", [P, 1])
        bv_bc, bo_bc, s3_bc = (sb(n, [P, D]) for n in ("bv_bc", "bo_bc", "s3_bc"))
        s_sb = {n: sb(f"{n}_sb", [P, MT]) for n in ("w1s", "w2s", "h1s", "h2s")}
        ident, ident_bf = sb("ident", [P, P]), sb("ident_bf", [P, P], BF16)

        arena = [sb(f"arena{n}", [P, PARTS * MT * TOK], BF16) for n in range(2)]
        hid = [a[:, :].rearrange("p (i m t) -> p i m t", i=PARTS, m=MT) for a in arena]
        qk = arena[0][:, 0:4 * HG * L]
        qx = qk[:, 0:2 * HG * L].rearrange("p (s c h t) -> p s c h t", s=2, c=QC, h=HG)
        kx = qk[:, 2 * HG * L:4 * HG * L].rearrange("p (s h t) -> p s h t", s=2, h=HG)
        proj = arena[0][:, 4 * HG * L:].bitcast(F32).rearrange("p (n c) -> p n c", c=C)
        attn = arena[1][:, 0:2 * U_ALL * C].bitcast(F32).rearrange("p (u c) -> p u c", c=C)
        probs = arena[1][:, 2 * U_ALL * C:].bitcast(F32).rearrange("p (s h c) -> p s h c", s=2, h=HG)
        prt = sb("prt", [P, 2 * PARTS * TOK], BF16)
        part = {n: prt[:, a * PARTS * TOK:(a + 1) * PARTS * TOK].rearrange("p (i t) -> p i t", i=PARTS)
                for a, n in enumerate("qk")}
        den = prt[:, 0:2 * TOK].bitcast(F32)
        x1T = prt[:, 2 * TOK:5 * TOK].rearrange("p (i t) -> p i t", i=PARTS)
        gate = prt[:, 5 * TOK:6 * TOK].bitcast(F32).rearrange("p (s c) -> p s c", s=2)
        attn_c = xT_sb
        den_c = [sb(f"den_c{n}", [P, 16 * k]) for n, k in enumerate((8, 6, 1, 1))]
        v_sb = sb("v_sb", [P, G_ALL, KT, HG * DH])
        v_pad = sb("v_pad", [P, 2, KT, HG, 32])
        negmax = sb("negmax", [P, 2, TURNS])
        zeros = sb("zeros", [P, TURNS])
        mrest = sb("mrest", [P, TURNS])
        mpart = sb("mpart", [P, 2, P // TURNS, TURNS], BF16)
        mT = sb("mT", [P, 2, P], BF16)
        x1 = v_sb[:, :, :, :].rearrange("p g k e -> p (g k e)").rearrange("p (t d) -> p t d", d=D)
        hf = sb("hf", [P, RING, C])
        nonzero = hf[:, :, :].rearrange("p n c -> p (n c)").bitcast(BF16)\
            .rearrange("p (n c) -> p n c", c=HID)
        ones = sb("ones", [P, 1], BF16)
        inexact = sb("inexact", [1, 1], mybir.dt.int32)
        z = sb("z", [P, 2, TILES, D])
        xr = z[:, :, :, :].rearrange("p s t d -> p s (t d)")
        any_more = sb("any_more", [1, 1])
        warmed = sb("warmed", [P, 1])
        stats, mv = sb("stats", [P, TILES, 6]), sb("mv", [P, 2, TILES, 2])
        veps, rstd, power = sb("veps", [P, 2, TILES]), sb("rstd", [P, 2, TILES]), sb("power", [P, TILES])
        ps = ctx.enter_context(nc.psum_tensor("ps", [P, 8, C], F32))
        ps_t = ps[:, T_BANK, :].bitcast(BF16)[:, 0:P]

        in_x = [sem(f"in_x{c}") for c in range(NC_)]
        in_k, in_q, in_v = sem("in_k"), sem("in_q"), sem("in_v")
        in_bk, in_bq = sem("in_bk"), sem("in_bq")
        in_mid = sem("in_mid")
        in_ffn = sem("in_ffn")
        zeros_set = sem("zeros_set")
        rows_set = sem("rows_set")
        ones_set = sem("ones_set")
        ident_ready = sem("ident_ready")
        job_done = sem("job_done")
        v_proj = sem("v_proj")
        proj_ready = sem("proj_ready")
        split_act = sem("split_act")
        split_dve = sem("split_dve")
        split_q0 = sem("split_q0")
        split_pool = sem("split_pool")
        v_ready = sem("v_ready")
        k_out = [sem(f"k_out{b}") for b in range(B)]
        q_out = [sem(f"q_out{c}") for c in range(NC_)]
        rows_in = [[sem(f"rows_in{s}{c}") for c in range(QC)] for s in range(2)]
        v_staged = sem("v_staged")
        max_scores = sem("max_scores")
        max_taken = sem("max_taken")
        msplit_step = sem("msplit_step")
        max_split = sem("max_split")
        max_turned = sem("max_turned")
        max_copied = sem("max_copied")
        mrow_in = [sem(f"mrow_in{s}") for s in range(2)]
        scores = sem("scores")
        exp_done = sem("exp_done")
        pv_done = sem("pv_done")
        unit_out = sem("unit_out")
        moved = [sem(f"moved{n}") for n in range(len(MOVES))]
        den_in = [sem(f"den_in{n}") for n in range(len(MOVES))]
        den_ready = sem("den_ready")
        den_out = sem("den_out")
        den_back = [sem(f"den_back{n}") for n in range(len(MOVES))]
        xres_ready = sem("xres_ready")
        in_w = sem("in_w")
        w_step = sem("w_step")
        flagged = sem("flagged")
        counted = sem("counted")
        inexact_set = sem("inexact_set")
        chunk_normed = sem("chunk_normed")
        wo_done = sem("wo_done")
        z_step = sem("z_step")
        z_ready = sem("z_ready")
        stats_ready = sem("stats_ready")
        var_ready = sem("var_ready")
        pow_step = sem("pow_step")
        rstd_ready = sem("rstd_ready")
        x1_ready = sem("x1_ready")
        x1_turned = sem("x1_turned")
        x1_split = sem("x1_split")
        x1T_ready = sem("x1T_ready")
        tile_mm = sem("tile_mm")
        tile_act = sem("tile_act")
        gated = sem("gated")
        part1 = sem("part1")
        left1 = sem("left1")
        part2 = sem("part2")
        hid_ready = sem("hid_ready")
        w3_done = sem("w3_done")
        out_ready = sem("out_ready")
        out_in = sem("out_in")

        block = ctx.enter_context(nc.Block())

        @block.sync
        def _(sp):
            xT_c = xT.rearrange("p (c t) -> c p t", c=NC_)
            sp.dma_start(xT_sb[:, 0:C], xT_c[0]).then_inc(in_x[0], 16)
            sp.dma_start(bk_sb[:], bk).then_inc(in_bk, 16)
            sp.dma_start(xT_sb[:, C:2 * C], xT_c[1]).then_inc(in_x[1], 16)
            sp.dma_start(bq_sb[:], bq).then_inc(in_bq, 16)
            sp.dma_start(wv_sb[:], wvT).then_inc(in_v, 16)
            for c in range(2, NC_):
                sp.dma_start(xT_sb[:, c * C:(c + 1) * C], xT_c[c]).then_inc(in_x[c], 16)
            sp.dma_start(bv_bc[:], bv.partition_broadcast(P)).then_inc(in_v, 16)

            def store_k(b, i):
                sp.dma_start(k_dram[i, :, b * NG:(b + 1) * NG].rearrange("d g h t -> (g h) d t"),
                             part["k"][:, i, b * L:(b + 1) * L]).then_inc(k_out[b], 16)

            def store_q(c, i):
                b, qc = c // QC, c % QC
                sp.dma_start(q_dram[i, :, qc, b * NG:(b + 1) * NG].rearrange("d g h t -> (g h) d t"),
                             part["q"][:, i, c * C:(c + 1) * C]).then_inc(q_out[c], 16)

            def load_k(g, slot):
                src = k_dram[:, :, bass.ds(g, 1)].rearrange("j d o h t -> o (j d) (h t)")
                sp.dma_start(kx[0:ROWS, slot].rearrange("r h t -> r (h t)"),
                             src.broadcast_to([PARTS, PARTS * DH, HG * L])).then_inc(rows_in[slot][0], 16)

            def load_q(g, slot, qc):
                for i in range(PARTS):
                    r = slice(DH * PARTS * i, DH * PARTS * (i + 1))
                    src = q_dram[i, :, qc, bass.ds(g, 1)].rearrange("d o h t -> o d (h t)")
                    sp.dma_start(qx[r, slot, qc].rearrange("r h t -> r (h t)"),
                                 src.broadcast_to([PARTS, DH, HG * C])).then_inc(rows_in[slot][qc], 16)

            def load_rows(g, slot):
                load_k(g, slot)
                load_q(g, slot, 0)
                load_q(g, slot, 1)

            def load_max(i, w):
                slot, qc = w // QC % 2, w % QC
                sp.wait_ge(max_copied, i * PER + w + 1)
                sp.dma_start(qx[ROWS:MROWS, slot, qc, :, :].rearrange("i h t -> i (h t)"),
                             mT[0:PARTS * TURNS, w % 2, :]).then_inc(mrow_in[w % 2], 16)

            sp.wait_ge(rows_set, 1)
            for i in range(PARTS):
                if i == 0:
                    sp.wait_ge(split_act, 2)
                else:
                    sp.wait_ge(split_dve, 4 + i)
                store_k(0, i)
            for i in range(PARTS):
                if i > 0:
                    sp.wait_ge(split_q0, 1 + i)
                else:
                    sp.wait_ge(split_act, 3)
                store_q(0, i)
            sp.wait_ge(k_out[0], STORE_INC)
            load_k(0, 0)
            sp.wait_ge(q_out[0], STORE_INC)
            load_q(0, 0, 0)
            sp.wait_ge(split_dve, 3 * 3)
            for i in range(PARTS):
                store_q(1, i)
            sp.wait_ge(q_out[1], STORE_INC)
            load_q(0, 0, 1)
            sp.wait_ge(rows_set, 2)
            load_rows(1, 1)
            load_max(0, 0)
            sp.wait_ge(split_pool, 2 * 3)
            for i in range(PARTS):
                store_k(1, i)
            for c in range(QC):
                sp.wait_ge(split_pool, (3 + c) * 3)
                for i in range(PARTS):
                    store_q(QC + c, i)
            sp.wait_ge(k_out[1], STORE_INC)
            for c in (2, 3):
                sp.wait_ge(q_out[c], STORE_INC)

            for dst, src in ((w_sb[:, SLICE["w1"], :], w1T), (w_sb[:, SLICE["w2"], :], w2T),
                             (w_sb[:, SLICE["h1"]:SLICE["h1"] + MT, :], h1T.rearrange("(k p) o -> p k o", p=P)),
                             (w_sb[:, SLICE["h2"]:SLICE["h2"] + MT, :], h2T.rearrange("(k p) o -> p k o", p=P)),
                             (w_sb[:, SLICE["w3"], :].rearrange("p (k o) -> p k o", k=MT),
                              w3T.rearrange("(k p) o -> p k o", p=P))):
                sp.dma_start(dst, src).then_inc(in_w, 16)

            with sp.Fori(0, ITERS - 1) as i:
                load_max(i, 1)
                load_max(i, 2)
                sp.wait_ge(scores, i * (STEPS * HG) + STEPS * HG // 2)
                load_rows(i * 2 + 2, 0)
                load_max(i, 3)
                load_max(i, 4)
                sp.wait_ge(scores, i * (STEPS * HG) + STEPS * HG)
                load_rows(i * 2 + 3, 1)
            sp.dma_start(xres[:], x.rearrange("(t p) d -> p t d", p=P)).then_inc(in_mid, 16)
            sp.dma_start(bo_bc[:], bo.partition_broadcast(P)).then_inc(in_mid, 16)
            sp.dma_start(wo_sb[:], woT).then_inc(in_mid, 16)
            for dst, src in ((s3_bc[:], w3s.partition_broadcast(P)),
                             (s_sb["w1s"][:], w1s), (s_sb["w2s"][:], w2s),
                             (s_sb["h1s"][:], h1s), (s_sb["h2s"][:], h2s)):
                sp.dma_start(dst, src).then_inc(in_ffn, 16)

            def gather(n):
                b, u0, u1 = MOVES[n]
                sp.wait_ge(unit_out, b * 8 + u1)
                for j in range(HG):
                    row = attn[32 * j + DH:32 * j + DH + 1, b * 8 + u0:b * 8 + u1, :]
                    sp.dma_start(den_c[n][32 * j:32 * j + 32, :],
                                 row.rearrange("o u c -> o (u c)").rearrange("o (x y) -> o x y", x=32))\
                      .then_inc(den_in[n], 16)

            def spread(n):
                b, u0, u1 = MOVES[n]
                sp.wait_ge(den_ready, n + 1)
                g0, g1 = u0 // QC, (u1 + QC - 1) // QC
                t0, t1 = (0, L) if u1 - u0 >= QC else (u0 % QC * C, u0 % QC * C + C)
                dram = den_dram[b, :, g0:g1, t0:t1]
                sp.dma_start(dram, den_c[n][:, :]).then_inc(den_out, 16)
                sp.wait_ge(den_out, 16 * n + 16)
                for g in range(g0, g1):
                    sp.dma_start(den[g * HG * DH:(g + 1) * HG * DH, b * L + t0:b * L + t1],
                                 dram[:, g - g0].unsqueeze(1).broadcast_to([HG, DH, t1 - t0]))\
                      .then_inc(den_back[n], 16)

            def move(n):
                b, u0, u1 = MOVES[n]
                sp.wait_ge(unit_out, b * 8 + u1)
                for g in range(u0 // QC, (u1 + QC - 1) // QC):
                    q0, q1 = max(u0, g * QC), min(u1, g * QC + QC)
                    for j in range(HG):
                        sp.dma_start(attn_c[(g * HG + j) * DH:(g * HG + j + 1) * DH,
                                            b * L + (q0 - g * QC) * C:b * L + (q1 - g * QC) * C],
                                     attn[32 * j:32 * j + DH, b * 8 + q0:b * 8 + q1, :]
                                     .rearrange("d u c -> d (u c)")).then_inc(moved[n], 16)

            load_max(ITERS - 1, 1)
            gather(0)
            move(0)
            load_max(ITERS - 1, 2)
            spread(0)
            load_max(ITERS - 1, 3)
            gather(1)
            move(1)
            spread(1)
            gather(2)
            move(2)
            spread(2)
            gather(3)
            move(3)
            spread(3)
            out_t = out.rearrange("(t p) d -> p t d", p=P)

            def store(n, c, t0, t1):
                sp.wait_ge(out_ready, n + 1)
                at = bass.ds(c * TILES + t0, t1 - t0)
                sp.dma_start(out_t[:, at, :], xres[:, at, :]).then_inc(out_in, 16)

            with sp.Fori(0, NC_ - 1) as c:
                store(c, c, 0, TILES)
            for n, (c, t0, t1) in enumerate(PIECES):
                store(n + NC_ - 1, c, t0, t1)
            sp.wait_ge(out_in, 16 * (NC_ - 1 + len(PIECES)))

        @block.scalar
        def _(act):
            act.dma_start(wk_sb[:], wkT).then_inc(in_k, 16)
            act.dma_start(wq_sb[:], wqT).then_inc(in_q, 16)

            def warm(func):
                nc.scalar.activation(warmed[:], zeros[:, 0:1], func)

            act.wait_ge(zeros_set, 1)
            warm(ACT.Exp)
            act.wait_ge(in_bk, 16)
            for n, (name, c) in enumerate(JOBS):
                if n == 2:
                    act.wait_ge(in_bq, 16)
                act.wait_ge(job_done, n + 1)
                nc.scalar.activation(proj[:, n, :], ps[:, JOB_BANKS[n % 4], :], ACT.Identity,
                                     bias=(bq_sb if name == "q" else bk_sb)[:, 0:1]).then_inc(proj_ready, 1)
                act.wait_ge(proj_ready, n + 1)
                nc.scalar.activation(part[name][:, 0, c * C:(c + 1) * C], proj[:, n, :],
                                     ACT.Copy).then_inc(split_act, 1)

            def exps(i, k, heads=range(HG)):
                for h in heads:
                    act.wait_ge(scores, i * (STEPS * HG) + k * HG + h + 1)
                    nc.scalar.activation(probs[:, k % 2, h, :], ps[:, ST_BANK[h], :], ACT.Exp,
                                         scale=SCALE).then_inc(exp_done, 1)

            attn_flat = arena[1][:, 0:2 * U_ALL * C].bitcast(F32)

            def copy_max(i, w):
                act.wait_ge(max_turned, i * PER + w + 1)
                nc.scalar.activation(mT[:, w % 2, :], ps_t, ACT.Copy).then_inc(max_copied, 1)

            def units(i, last):
                for k in range(STEPS):
                    if not (last and k == STEPS - 1):
                        exps(i, k + 1, (0, 1, 2))
                    if k % KT == KT - 1:
                        act.wait_ge(pv_done, i * STEPS + k + 1)
                        nc.scalar.activation(attn_flat[:, bass.ds(i * (PER * C) + k // KT * C, C)],
                                             ps[:, PV_BANK, :], ACT.Copy).then_inc(unit_out, 1)
                    if not (last and k == STEPS - 1):
                        exps(i, k + 1, (3,))
                    if k % KT == TSTEP and not (last and k // KT == PER - 1):
                        copy_max(i, k // KT + 1)

            copy_max(0, 0)
            exps(0, 0)
            with act.Fori(0, ITERS - 1) as i:
                units(i, False)
            units(ITERS - 1, True)

            def first(order, name, c, m):
                at = order * MT + m
                act.wait_ge(tile_mm, at + 1)
                if name == "gate":
                    if c > 0 or m >= 2:
                        act.wait_ge(gated, c * MT + m - 1)
                    nc.scalar.activation(gate[:, m % 2, :], ps[:, GATE_BANK + 2 * (m % 2), :], ACT.Silu,
                                         scale=s_sb["w1s"][:, m:m + 1]).then_inc(tile_act, 1)
                else:
                    act.wait_ge(hid_ready, at - RING + 1)
                    nc.scalar.activation(hf[:, m % RING, :], ps[:, GELU_BANK + m % 2, :], ACT.Gelu,
                                         scale=s_sb[name + "s"][:, m:m + 1]).then_inc(tile_act, 1)

            def second(order, name, c, m):
                if name == "gate":
                    act.wait_ge(gated, c * MT + m + 1)
                else:
                    act.wait_ge(tile_act, order * MT + m + 1)
                nc.scalar.activation(hid[name == "h1"][:, 0, m, bass.ds(c * C, C)], hf[:, m % RING, :],
                                     ACT.Copy).then_inc(part1, 1)

            def third(order, name, c, m):
                act.wait_ge(left1, order * MT + m + 1)
                nc.scalar.activation(hid[name == "h1"][:, 1, m, bass.ds(c * C, C)], hf[:, m % RING, :],
                                     ACT.Copy).then_inc(part2, 1)

            def steps(tiles, arena_from=None):
                for n in range(len(tiles) + 2):
                    if n < len(tiles):
                        if n == arena_from:
                            for k in range(len(MOVES)):
                                act.wait_ge(moved[k], MOVED[k])
                                act.wait_ge(den_in[k], 64)
                        first(*tiles[n])
                    if 0 <= n - 1 < len(tiles):
                        second(*tiles[n - 1])
                    if n >= 2:
                        third(*tiles[n - 2])
                    if n + 1 < len(tiles) and tiles[n + 1][1] != tiles[n][1]:
                        warm(ACT.Silu if tiles[n + 1][1] == "gate" else ACT.Gelu)

            warm(ACT.Silu)
            act.wait_ge(in_ffn, 80)
            steps([(order, name, c, m) for order, (name, c) in enumerate(ORDER[0:6]) for m in range(MT)],
                  ORDER.index(("h1", 0)) * MT)
            warm(ACT.Gelu)
            with act.Fori(2, NC_) as c:
                steps([(c + 4, "h1", c, m) for m in range(MT)])
            with act.Fori(0, NC_) as c:
                steps([(c + 8, "h2", c, m) for m in range(MT)])

        @block.gpsimd
        def _(pool):
            nc.gpsimd.memset(zeros[:], 0.0).then_inc(zeros_set, 1)
            nc.gpsimd.memset(ones[:], 1.0).then_inc(ones_set, 1)
            none = zeros[:, 0:1].broadcast_to([P, C])

            def split(n, steps, done):
                name, c = JOBS[n]
                at = slice(c * C, (c + 1) * C)
                pool.wait_ge(split_act, n + 1)
                nc.gpsimd.tensor_tensor(proj[:, n, :], proj[:, n, :], part[name][:, 0, at],
                                        ALU.subtract).then_inc(steps, 1)
                pool.wait_ge(steps, done + 1)
                nc.gpsimd.tensor_tensor(part[name][:, 1, at], proj[:, n, :], none, ALU.add).then_inc(steps, 1)
                pool.wait_ge(steps, done + 2)
                nc.gpsimd.tensor_tensor(part[name][:, 2, at], proj[:, n, :], part[name][:, 1, at],
                                        ALU.subtract).then_inc(steps, 1)

            nc.gpsimd.memset(ident[:], 1.0).then_inc(ident_ready, 1)
            pool.wait_ge(ident_ready, 1)
            nc.gpsimd.affine_select(out=ident[:], in_=ident[:], compare_op=ALU.is_equal, fill=0.0, base=0,
                                    pattern=[[-1, P]], channel_multiplier=1).then_inc(ident_ready, 1)
            pool.wait_ge(ident_ready, 2)
            nc.gpsimd.tensor_copy(ident_bf[:], ident[:]).then_inc(ident_ready, 1)
            split(2, split_q0, 0)
            nc.gpsimd.memset(power[:], -0.5).then_inc(ones_set, 1)
            nc.gpsimd.memset(v_pad[:], 1.0).then_inc(ones_set, 1)
            nc.gpsimd.memset(mpart[:], 0.0).then_inc(ones_set, 1)
            pool.wait_ge(ones_set, 4)

            def stage_v(g, slot):
                nc.gpsimd.tensor_copy(
                    v_pad[:, slot, :, :, 0:DH],
                    v_sb[:, :, :, :].rearrange("p g k (h d) -> p (g k) h d", h=HG)[:, bass.ds(g * KT, KT), :, :]
                ).then_inc(v_staged, 1)

            def split_max(i, w):
                m, parts = negmax[:, w % 2, :], mpart[:, w % 2, :, :]
                done = i * (3 * PER) + 3 * w
                pool.wait_ge(max_taken, i * (PER * TURNS) + w * TURNS + TURNS)
                nc.gpsimd.tensor_tensor(parts[:, 0, :], m, zeros[:], ALU.add).then_inc(msplit_step, 1)
                pool.wait_ge(msplit_step, done + 1)
                nc.gpsimd.tensor_tensor(mrest[:], m, parts[:, 0, :], ALU.subtract).then_inc(msplit_step, 1)
                pool.wait_ge(msplit_step, done + 2)
                nc.gpsimd.tensor_tensor(parts[:, 1, :], mrest[:], zeros[:], ALU.add)\
                  .then_inc(msplit_step, 1)
                pool.wait_ge(msplit_step, done + 3)
                nc.gpsimd.tensor_tensor(parts[:, 2, :], mrest[:], parts[:, 1, :], ALU.subtract)\
                  .then_inc(max_split, 1)

            split(4, split_pool, 0)
            split(5, split_pool, 3)
            pool.wait_ge(v_ready, 2)
            stage_v(0, 0)
            stage_v(1, 1)
            split_max(0, 0)
            split(6, split_pool, 6)
            split(7, split_pool, 9)
            pool.wait_ge(v_ready, NC_)

            def split_w(n):
                w, first, second, third = w_sb[:, n, :], w_first[:, n, :], w_more[:, n, 0, :], w_more[:, n, 1, :]
                nc.gpsimd.tensor_tensor(first, w, none, ALU.add).then_inc(w_step, 1)
                pool.wait_ge(w_step, n * 4 + 1)
                nc.gpsimd.tensor_tensor(w_left[:], w, first, ALU.subtract).then_inc(w_step, 1)
                pool.wait_ge(w_step, n * 4 + 2)
                nc.gpsimd.tensor_tensor(second, w_left[:], none, ALU.add).then_inc(w_step, 1)
                pool.wait_ge(w_step, n * 4 + 3)
                nc.gpsimd.tensor_tensor(third, w_left[:], second, ALU.subtract).then_inc(w_step, 1)
                pool.wait_ge(w_step, n * 4 + 4)

            with pool.Fori(0, ITERS - 1) as i:
                split_max(i, 1)
                split_max(i, 2)
                pool.wait_ge(pv_done, i * STEPS + STEPS // 2)
                stage_v(i * 2 + 2, 0)
                split_max(i, 3)
                split_max(i, 4)
                pool.wait_ge(pv_done, i * STEPS + STEPS)
                stage_v(i * 2 + 3, 1)
            def rstds(n, slot, k):
                pool.wait_ge(var_ready, n + 1)
                nc.gpsimd.tensor_scalar(veps[:, slot, 0:k], mv[:, slot, 0:k, 1], EPS, None, ALU.add)\
                  .then_inc(pow_step, 1)
                pool.wait_ge(pow_step, n + 1)
                nc.gpsimd.tensor_tensor(rstd[:, slot, 0:k], veps[:, slot, 0:k], power[:, 0:k], ALU.pow)\
                  .then_inc(rstd_ready, 1)

            def third_x1(c):
                pool.wait_ge(x1_split, 3 * c + 3)
                nc.gpsimd.tensor_tensor(x1T[:, 2, c * C:(c + 1) * C], xr[:, c % 2, :],
                                        x1T[:, 1, c * C:(c + 1) * C], ALU.subtract).then_inc(x1T_ready, 1)

            def thirds(order, name, c):
                dst = hid[name == "h1"]
                for m in range(MT):
                    pool.wait_ge(part2, order * MT + m + 1)
                    nc.gpsimd.tensor_tensor(dst[:, 2, m, bass.ds(c * C, C)], hf[:, m % RING, :],
                                            dst[:, 1, m, bass.ds(c * C, C)], ALU.subtract)\
                      .then_inc(hid_ready, 1)

            pool.wait_ge(in_w, 80)
            for w in range(PER):
                if w > 0:
                    split_max(ITERS - 1, w)
                if w == 1:
                    pool.wait_ge(in_mid, 48)
                    nc.gpsimd.tensor_tensor(xres[:], xres[:],
                                            bo_bc[:, :].unsqueeze(1).broadcast_to([P, TOK // P, D]),
                                            ALU.add).then_inc(xres_ready, 1)
                for n in range(sum(WINDOWS[0:w]), sum(WINDOWS[0:w + 1])):
                    split_w(n)
            for c in (0, 1):
                rstds(c, c % 2, TILES)
            for c in (0, 1):
                third_x1(c)
            thirds(0, "gate", 0)
            thirds(1, "gate", 1)
            for c in (2, 3):
                rstds(c, c % 2, TILES)
            thirds(2, "h1", 0)
            third_x1(2)
            third_x1(3)
            thirds(3, "h1", 1)
            thirds(4, "gate", 2)
            thirds(5, "gate", 3)
            with pool.Fori(2, NC_) as c:
                thirds(c + 4, "h1", c)
            thirds(8, "h2", 0)
            for c in range(1, NC_):
                thirds(c + 8, "h2", c)
                rstds(c + (NC_ - 1), 0, TILES)
            for n, (c, t0, t1) in enumerate(PIECES):
                rstds(n + 2 * NC_ - 1, 1 - n % 2, t1 - t0)

        @block.vector
        def _(dve):
            nc.vector.memset(kx[64:MROWS, 0, :, :], 1.0).then_inc(rows_set, 1)

            def split(n):
                name, c = JOBS[n]
                at = slice(c * C, (c + 1) * C)
                done = 3 * DVE_JOBS.index(n)
                dve.wait_ge(split_act, n + 1)
                nc.vector.tensor_tensor(proj[:, n, :], proj[:, n, :], part[name][:, 0, at],
                                        ALU.subtract).then_inc(split_dve, 1)
                dve.wait_ge(split_dve, done + 1)
                nc.vector.tensor_copy(part[name][:, 1, at], proj[:, n, :]).then_inc(split_dve, 1)
                dve.wait_ge(split_dve, done + 2)
                nc.vector.tensor_tensor(part[name][:, 2, at], proj[:, n, :], part[name][:, 1, at],
                                        ALU.subtract).then_inc(split_dve, 1)

            for n in DVE_JOBS:
                split(n)
            nc.vector.memset(kx[64:MROWS, 1, :, :], 1.0).then_inc(rows_set, 1)
            dve.wait_ge(in_v, 32)
            for c in range(NC_):
                dve.wait_ge(v_proj, c + 1)
                b, k0 = c // (NC_ // B), (c % (NC_ // B)) * TILES
                nc.vector.tensor_tensor(
                    v_sb[:, b * NG:(b + 1) * NG, k0:k0 + TILES, :],
                    ps[:, MAX_BANK + c, :].rearrange("p (t g e) -> p g t e", t=TILES, g=NG),
                    bv_bc[:, :].rearrange("p (g e) -> p g e", g=NG).unsqueeze(2)
                    .broadcast_to([P, NG, TILES, HG * DH]),
                    ALU.add).then_inc(v_ready, 1)

            def turn(i, t):
                dve.wait_ge(max_scores, i * (PER * TURNS) + t + 1)
                if t % TURNS == 0 and t >= 2 * TURNS:
                    dve.wait_ge(max_split, i * PER + t // TURNS - 1)
                bank = MAX_BANK + 2 * (t % 2)
                nc.vector.tensor_reduce(negmax[:, t // TURNS % 2, t % TURNS:t % TURNS + 1],
                                        ps[:, bank:bank + 2, :], AX.XY, ALU.max, negate=True)\
                  .then_inc(max_taken, 1)

            for t in range(TURNS + LEAD):
                turn(0, t)

            with dve.Fori(0, ITERS - 1) as i:
                for k in range(STEPS):
                    turn(i, TURNS + LEAD + 2 * k)
                    turn(i, TURNS + LEAD + 2 * k + 1)

            def invert(n):
                dve.wait_ge(den_in[n], 64)
                nc.vector.reciprocal(den_c[n][:], den_c[n][:]).then_inc(den_ready, 1)

            def norm(c):
                if c == 0:
                    dve.wait_ge(den_back[0], 16 * NG)
                    dve.wait_ge(moved[0], MOVED[0])
                if c == QC:
                    dve.wait_ge(den_back[1], 16 * (NG - 1))
                    dve.wait_ge(moved[1], MOVED[1])
                if c >= QC:
                    dve.wait_ge(den_back[c], 16)
                    dve.wait_ge(moved[c], MOVED[c])
                at = slice(c * C, (c + 1) * C)
                nc.vector.tensor_tensor(attn_c[:, at], attn_c[:, at], den[:, at], ALU.mult)\
                  .then_inc(chunk_normed, 1)

            def flag(n0, n1):
                dve.wait_ge(w_step, 4 * n1)
                nc.vector.tensor_scalar(nonzero[:, 0:n1 - n0, :], w_more[:, n0:n1, 0, :], 0.0, None,
                                        ALU.not_equal).then_inc(flagged, 1)

            def statistics(n, slot, psum, add, scaled=False):
                tiles = add.shape[1]
                zc = z[:, slot, 0:tiles]
                psum = psum.rearrange("p (t d) -> p t d", t=tiles)
                if scaled:
                    nc.vector.tensor_tensor(zc, psum, s3_bc[:, :].unsqueeze(1).broadcast_to([P, tiles, D]),
                                            ALU.mult).then_inc(z_step, 1)
                    dve.wait_ge(z_step, n - (NC_ - 1))
                nc.vector.tensor_tensor(zc, zc if scaled else psum, add, ALU.add).then_inc(z_ready, 1)
                dve.wait_ge(z_ready, n + 1)
                for t in range(tiles):
                    ins = nc.vector.bn_stats(stats[:, t, :], zc[:, t, :])
                ins.then_inc(stats_ready, 1)
                dve.wait_ge(stats_ready, n + 1)
                for t in range(tiles):
                    ins = nc.vector.bn_aggr(mv[:, slot, t, :], stats[:, t, :])
                ins.then_inc(var_ready, 1)

            def normalize(n, slot, dst):
                dve.wait_ge(rstd_ready, n + 1)
                for t in range(dst.shape[1]):
                    ins = nc.vector.tensor_scalar(dst[:, t, :], z[:, slot, t, :], mv[:, slot, t, 0:1],
                                                  rstd[:, slot, t:t + 1], ALU.subtract, ALU.mult)
                return ins

            def first_stats(c):
                dve.wait_ge(wo_done, c + 1)
                if c == 0:
                    dve.wait_ge(xres_ready, 1)
                if c >= 2:
                    dve.wait_ge(x1T_ready, c - 1)
                statistics(c, c % 2, ps[:, WO_BANK[c], :], xres[:, c * TILES:(c + 1) * TILES, :])

            def first_apply(c):
                if c == 0:
                    dve.wait_ge(v_staged, G_ALL)
                normalize(c, c % 2, x1[:, c * TILES:(c + 1) * TILES, :]).then_inc(x1_ready, 1)

            def split_x1(c):
                at = slice(c * C, (c + 1) * C)
                bank = ps[:, X1T_BANK[c], :]
                dve.wait_ge(x1_turned, c + 1)
                nc.vector.tensor_copy(x1T[:, 0, at], bank).then_inc(x1_split, 1)
                dve.wait_ge(x1_split, 3 * c + 1)
                nc.vector.tensor_tensor(xr[:, c % 2, :], bank, x1T[:, 0, at], ALU.subtract)\
                  .then_inc(x1_split, 1)
                dve.wait_ge(x1_split, 3 * c + 2)
                nc.vector.tensor_copy(x1T[:, 1, at], xr[:, c % 2, :]).then_inc(x1_split, 1)

            def gate_tile(order, c, m):
                at = order * MT + m
                dve.wait_ge(tile_act, at + 1)
                if order > 0:
                    dve.wait_ge(hid_ready, at - RING + 1)
                nc.vector.scalar_tensor_tensor(
                    out=hf[:, m % RING, :], in0=ps[:, GATE_BANK + 2 * (m % 2) + 1, :],
                    scalar=s_sb["w2s"][:, m:m + 1], in1=gate[:, m % 2, :],
                    op0=ALU.mult, op1=ALU.mult).then_inc(gated, 1)

            def leave(order, name, c, m):
                dve.wait_ge(part1, order * MT + m + 1)
                nc.vector.tensor_tensor(hf[:, m % RING, :], hf[:, m % RING, :],
                                        hid[name == "h1"][:, 0, m, bass.ds(c * C, C)], ALU.subtract)\
                  .then_inc(left1, 1)

            def steps(chunks, between={}):
                tiles = [(order, name, c, m) for order, name, c in chunks for m in range(MT)]
                for n in range(len(tiles) + 1):
                    if n < len(tiles):
                        order, name, c, m = tiles[n]
                        if name == "gate":
                            gate_tile(order, c, m)
                    if n > 0:
                        leave(*tiles[n - 1])
                    if n in between:
                        between[n]()

            for k in range(STEPS):
                for t in (TURNS + LEAD + 2 * k, TURNS + LEAD + 2 * k + 1):
                    if t < PER * TURNS:
                        turn(ITERS - 1, t)
                if k == KT:
                    invert(0)
            norm(0)
            norm(1)
            flag(0, FLAGGED)
            first_stats(0)
            invert(1)
            first_apply(0)
            dve.wait_ge(counted, 1)
            flag(FLAGGED, SLICES)
            first_stats(1)
            dve.wait_ge(counted, 2)
            nc.vector.tensor_reduce(any_more[:], ps[0:1, INEXACT_BANK, :], AX.X, ALU.max)\
              .then_inc(flagged, 1)
            dve.wait_ge(flagged, 3)
            nc.vector.tensor_scalar(inexact[:], any_more[:], 0.0, None, ALU.is_gt).then_inc(inexact_set, 1)
            first_apply(1)
            split_x1(0)
            invert(2)
            split_x1(1)
            dve.wait_ge(in_ffn, 80)
            steps([(0, "gate", 0), (1, "gate", 1)], {MT: lambda: invert(3), MT + 2: lambda: norm(2)})
            norm(3)
            first_stats(2)
            first_stats(3)
            first_apply(2)
            first_apply(3)
            steps([(2, "h1", 0)])
            split_x1(2)
            split_x1(3)
            steps([(3, "h1", 1), (4, "gate", 2), (5, "gate", 3)])
            with dve.Fori(2, NC_) as c:
                steps([(c + 4, "h1", c)])
            def last_norm(n, slot, bank, c, t0, t1):
                dve.wait_ge(w3_done, n + 1)
                at = bass.ds(c * TILES + t0, t1 - t0)
                statistics(n + NC_, slot, ps[:, bank, 0:(t1 - t0) * P], x1[:, at, :], True)
                normalize(n + NC_, slot, xres[:, at, :]).then_inc(out_ready, 1)

            steps([(8, "h2", 0)])
            for c in range(1, NC_):
                steps([(c + 8, "h2", c)])
                last_norm(c - 1, 0, W3_BANK, c - 1, 0, TILES)
            for n, (c, t0, t1) in enumerate(PIECES):
                last_norm(n + NC_ - 1, 1 - n % 2, W3_BANK + 1 + n, c, t0, t1)

        @block.tensor
        def _(pe):
            for n, (name, c) in enumerate(JOBS):
                pe.wait_ge(in_x[c], 16)
                if n == 0:
                    pe.wait_ge(in_k, 16)
                if n == 2:
                    pe.wait_ge(in_q, 16)
                if n >= 4:
                    pe.wait_ge(proj_ready, n - 3)
                nc.tensor.matmul(ps[:, JOB_BANKS[n % 4], :], (wq_sb if name == "q" else wk_sb)[:],
                                 xT_sb[:, c * C:(c + 1) * C], start=True, stop=True).then_inc(job_done, 1)
                if n == 3:
                    pe.wait_ge(in_v, 32)
                    for c in range(NC_):
                        pe.wait_ge(in_x[c], 16)
                        for t in range(TILES):
                            ins = nc.tensor.matmul(ps[:, MAX_BANK + c, t * P:(t + 1) * P],
                                                   xT_sb[:, c * C + t * P:c * C + (t + 1) * P], wv_sb[:],
                                                   start=True, stop=True)
                        ins.then_inc(v_proj, 1)

            def turn(i, t, half):
                slot, qc, h, q = t // (QC * TURNS) % 2, t // TURNS % QC, t % TURNS // QT, t % QT
                if half == 0:
                    if t >= 2:
                        pe.wait_ge(max_taken, i * (PER * TURNS) + t - 1)
                    if t % TURNS == 0:
                        inc = LOAD_INC[qc]
                        pe.wait_ge(rows_in[slot][qc], i * inc + (t // (PER * TURNS) + 1) * inc)
                ins = nc.tensor.matmul(ps[:, MAX_BANK + 2 * (t % 2) + half, :],
                                       qx[0:ROWS, slot, qc, h, q * P:(q + 1) * P],
                                       kx[0:ROWS, slot, h, half * C:(half + 1) * C], start=True, stop=True)
                if half == 1:
                    ins.then_inc(max_scores, 1)

            def turn_max(i, w):
                pe.wait_ge(max_split, i * PER + w + 1)
                if w > 0:
                    pe.wait_ge(exp_done, i * (STEPS * HG) + ((w - 1) * KT + TSTEP + 1) * HG + 3)
                nc.tensor.transpose(ps_t, mpart[:, w % 2, :, :].rearrange("p i t -> p (i t)"), ident_bf[:])\
                  .then_inc(max_turned, 1)

            def score(i, k, h, last=False):
                w, kt = k // KT, k % KT
                slot, qc = w // QC % 2, w % QC
                if k > 0 or h == 3:
                    pe.wait_ge(exp_done, i * (STEPS * HG) + k * HG + (1 - HG, 0, 3 - HG, 2)[h])
                if h == 2 and kt == TSTEP + 2 and not (last and w == PER - 1):
                    pe.wait_ge(max_copied, i * PER + w + 2)
                if kt == 0 and h == 0:
                    pe.wait_ge(mrow_in[w % 2], i * (PER // 2 * MROW_INC) + (w // 2 + 1) * MROW_INC)
                nc.tensor.matmul(ps[:, ST_BANK[h], :], kx[0:MROWS, slot, h, kt * P:(kt + 1) * P],
                                 qx[0:MROWS, slot, qc, h, :], start=True, stop=True)\
                  .then_inc(scores, 1)

            def product(i, k):
                w, kt = k // KT, k % KT
                if kt == 0 and w % QC == 0:
                    pe.wait_ge(v_staged, i * (PER // QC) + w // QC + 1)
                pe.wait_ge(exp_done, i * (STEPS * HG) + k * HG + HG)
                for h in range(HG):
                    ins = nc.tensor.matmul(ps[32 * h:32 * h + 32, PV_BANK, :], v_pad[:, w // QC, kt, h, :],
                                           probs[:, k % 2, h, :], start=(kt == 0), stop=(kt == KT - 1),
                                           tile_position=(0, 32 * h))
                ins.then_inc(pv_done, 1)

            pe.wait_ge(v_ready, NC_)
            def busy(n):
                for _ in range(n):
                    nc.tensor.matmul(ps[:, PV_BANK, :], part["k"][:, 0, 0:P], part["k"][:, 0, 0:C],
                                     start=True, stop=True)

            for t in range(TURNS + LEAD):
                turn(0, t, 0)
                turn(0, t, 1)
                if t > TURNS + 2:
                    busy(1)
                if t == TURNS + 2:
                    pe.wait_ge(proj_ready, len(JOBS))
                    pe.wait_ge(ident_ready, 3)
                    turn_max(0, 0)
            busy(2)
            for h in range(HG):
                if h == 2:
                    pe.wait_ge(max_copied, 1)
                if h == 3:
                    busy(4)
                score(0, 0, h)
            busy(3)

            def out_proj(c):
                pe.wait_ge(chunk_normed, c + 1)
                if c == 0:
                    pe.wait_ge(in_mid, 48)
                    pe.wait_ge(max_taken, U_ALL * TURNS)
                if c == 2:
                    pe.wait_ge(unit_out, U_ALL)
                for t in range(TILES):
                    at = slice(c * C + t * P, c * C + (t + 1) * P)
                    ins = nc.tensor.matmul(ps[:, WO_BANK[c], t * P:(t + 1) * P], attn_c[:, at], wo_sb[:],
                                           start=True, stop=True)
                ins.then_inc(wo_done, 1)

            def turn_x1(c):
                pe.wait_ge(x1_ready, c + 1)
                if X1T_BANK[c] == INEXACT_BANK:
                    pe.wait_ge(inexact_set, 1)
                for t in range(TILES):
                    ins = nc.tensor.transpose(ps[:, X1T_BANK[c], t * P:(t + 1) * P],
                                              x1[:, c * TILES + t, :], ident[:])
                ins.then_inc(x1_turned, 1)

            def count(n0, n1):
                pe.wait_ge(flagged, 1 if n0 == 0 else 2)
                for n in range(n0, n1):
                    ins = nc.tensor.matmul(ps[0:1, INEXACT_BANK, :], ones[:], nonzero[:, n - n0, :],
                                           start=(n == 0), stop=(n == SLICES - 1))
                ins.then_inc(counted, 1)

            BEHIND = {STEPS - 9: (out_proj, 0), STEPS - 8: (out_proj, 1),
                      STEPS - 7: (count, 0, FLAGGED), STEPS - 5: (count, FLAGGED, SLICES),
                      STEPS - 4: (turn_x1, 0), STEPS - 2: (turn_x1, 1)}

            def units(i, last):
                for k in range(STEPS):
                    more = not (last and k == STEPS - 1)
                    t = TURNS + LEAD + 2 * k
                    end = PER * TURNS if last else 2 * PER * TURNS
                    for h in (0, 1, 2):
                        if more:
                            score(i, k + 1, h, last)
                    product(i, k)
                    if t < end:
                        turn(i, t, 0)
                    if more:
                        score(i, k + 1, 3)
                    if t < end:
                        turn(i, t, 1)
                    if t + 1 < end:
                        turn(i, t + 1, 0)
                        turn(i, t + 1, 1)
                    if k % KT == TSTEP and not (last and k // KT == PER - 1):
                        turn_max(i, k // KT + 1)
                    if last and k in BEHIND:
                        stage, *of = BEHIND[k]
                        stage(*of)

            with pe.Fori(0, ITERS - 1) as i:
                units(i, False)
            units(ITERS - 1, True)

            pe.wait_ge(inexact_set, 1)
            more_parts = pe.value_load(inexact[0:1, 0:1], min_val=0, max_val=1)

            def product_sum(dst, ks, operands):
                def product(a, j, k, start, stop):
                    stationary, moving = operands(a, j, k)
                    return nc.tensor.matmul(dst, stationary, moving, start=start, stop=stop)

                for k in range(ks):
                    for j in range(PARTS):
                        if (k, j) != (ks - 1, PARTS - 1):
                            product(0, j, k, k + j == 0, False)
                with pe.If(more_parts > 0):
                    for a in range(1, PARTS):
                        for k in range(ks):
                            for j in range(PARTS):
                                product(a, j, k, False, False)
                return product(0, PARTS - 1, ks - 1, False, True)

            def weight(a, n, cols):
                return w_first[:, n, cols] if a == 0 else w_more[:, n, a - 1, cols]

            def gate_tile(c, m):
                if c > 0 or m >= 2:
                    pe.wait_ge(gated, c * MT + m - 1)
                cols, at = slice(m * P, (m + 1) * P), slice(c * C, (c + 1) * C)
                for n, name in enumerate(("w1", "w2")):
                    ins = product_sum(ps[:, GATE_BANK + 2 * (m % 2) + n, :], 1,
                                      lambda a, j, k: (weight(a, SLICE[name], cols), x1T[:, j, at]))
                ins.then_inc(tile_mm, 1)

            def gelu_tile(order, name, c, m):
                cols, src = slice(m * P, (m + 1) * P), hid[name == "h2"]
                pe.wait_ge(tile_act, order * MT + m - 1)
                product_sum(ps[:, GELU_BANK + m % 2, :], MT,
                            lambda a, j, k: (weight(a, SLICE[name] + k, cols), src[:, j, k, bass.ds(c * C, C)]))\
                    .then_inc(tile_mm, 1)

            for c in (0, 1):
                pe.wait_ge(x1T_ready, c + 1)
                for m in range(MT):
                    gate_tile(c, m)
            for c, stages in ((0, {1: (out_proj, 2), 2: (out_proj, 3)}), (1, {0: (turn_x1, 2), 1: (turn_x1, 3)})):
                pe.wait_ge(hid_ready, c * MT + MT)
                for m in range(MT):
                    gelu_tile(c + 2, "h1", c, m)
                    if m in stages:
                        stage, of = stages[m]
                        stage(of)
            for c in (2, 3):
                pe.wait_ge(x1T_ready, c + 1)
                for m in range(MT):
                    gate_tile(c, m)
            with pe.Fori(2, NC_) as c:
                pe.wait_ge(hid_ready, c * MT + 3 * MT)
                for m in range(MT):
                    gelu_tile(c + 4, "h1", c, m)
            def h2_chunk(c):
                pe.wait_ge(hid_ready, c * MT + 5 * MT)
                for m in range(MT):
                    gelu_tile(c + 8, "h2", c, m)

            def w3_products(c, bank, t0, t1):
                pe.wait_ge(hid_ready, c * MT + 9 * MT)
                for t in range(t0, t1):
                    at = bass.ds(c * C + t * P, P)
                    ins = product_sum(ps[:, bank, (t - t0) * P:(t - t0 + 1) * P], MT,
                                      lambda a, j, k: (hid[0][:, j, k, at],
                                                       weight(a, SLICE["w3"], slice(k * D, (k + 1) * D))))
                ins.then_inc(w3_done, 1)

            h2_chunk(0)
            h2_chunk(1)
            w3_products(0, W3_BANK, 0, TILES)
            with pe.Fori(2, NC_) as c:
                h2_chunk(c)
                pe.wait_ge(z_step, c - 1)
                w3_products(c - 1, W3_BANK, 0, TILES)
            for n, (c, t0, t1) in enumerate(PIECES):
                w3_products(c, W3_BANK + 1 + n, t0, t1)


def kernel(L0_attn_x, L0_attn_wq, L0_attn_bq, L0_attn_wk, L0_attn_bk, L0_attn_wv, L0_attn_bv,
           L0_attn_wo, L0_attn_bo, L0_ffn_w1_w, L0_ffn_w1_s, L0_ffn_w2_w, L0_ffn_w2_s,
           L0_ffn_h1_w, L0_ffn_h1_s, L0_ffn_h2_w, L0_ffn_h2_s, L0_ffn_w3_w, L0_ffn_w3_s):
    import numpy as np
    import concourse.bacc as bacc
    from concourse.bass_utils import run_bass_kernel_spmd

    def columns(v, n):
        return np.ascontiguousarray(np.asarray(v).reshape(n, -1).T)

    def turned(w):
        return np.ascontiguousarray(np.asarray(w).T)

    x = np.ascontiguousarray(np.asarray(L0_attn_x).reshape(TOK, D))
    arrays = {
        "xT": turned(x), "x": x,
        "wqT": turned(L0_attn_wq), "wkT": turned(L0_attn_wk), "wvT": turned(L0_attn_wv),
        "woT": turned(L0_attn_wo),
        "bq": columns(L0_attn_bq, 1), "bk": columns(L0_attn_bk, 1),
        "bv": np.ascontiguousarray(L0_attn_bv), "bo": np.ascontiguousarray(L0_attn_bo),
        "w1T": turned(L0_ffn_w1_w), "w2T": turned(L0_ffn_w2_w),
        "h1T": turned(L0_ffn_h1_w), "h2T": turned(L0_ffn_h2_w), "w3T": turned(L0_ffn_w3_w),
        "w1s": columns(L0_ffn_w1_s, MT), "w2s": columns(L0_ffn_w2_s, MT),
        "h1s": columns(L0_ffn_h1_s, MT), "h2s": columns(L0_ffn_h2_s, MT),
        "w3s": np.ascontiguousarray(L0_ffn_w3_s),
    }
    nc = bacc.Bacc("TRN2", target_bir_lowering=False, num_devices=1)
    args = {n: nc.dram_tensor(f"in_{n}", a.shape, F32, kind="ExternalInput").ap() for n, a in arrays.items()}
    k_dram = nc.dram_tensor("parts_k", (PARTS, DH, G_ALL, HG, L), BF16, kind="Internal").ap()
    q_dram = nc.dram_tensor("parts_q", (PARTS, DH, QC, G_ALL, HG, C), BF16, kind="Internal").ap()
    den_dram = nc.dram_tensor("den", (B, HG, NG, L), F32, kind="Internal").ap()
    out = nc.dram_tensor("out", (TOK, D), F32, kind="ExternalOutput").ap()
    build(nc, k_dram=k_dram, q_dram=q_dram, den_dram=den_dram, out=out, **args)
    r = run_bass_kernel_spmd(nc, [{f"in_{n}": a for n, a in arrays.items()}], core_ids=[0])
    return r.results[0]["out"].reshape(B, L, D)
```
